# Optimizing a Trainium2 kernel written in Bass

```python
import numpy as np
import jax
import jax.numpy as jnp

def _softmax(x, axis=-1):
    return jax.nn.softmax(x, axis=axis)

def _gelu(x):
    return jax.nn.gelu(x, approximate=True)

def _silu(x):
    return jax.nn.silu(x)

def _sigmoid(x):
    return jax.nn.sigmoid(x)

def _layernorm(x, axis=-1, eps=1e-05):
    m = jnp.mean(x, axis=axis, keepdims=True)
    v = jnp.var(x, axis=axis, keepdims=True)
    return (x - m) / jnp.sqrt(v + eps)

def _scatter_add(tgt, idx, src, axis=0):
    return tgt.at[idx].add(src)

def _segment_sum(src, seg, n):
    return jax.ops.segment_sum(src, seg, n)
kernel_name = 'mk_metaformer_d1_conv_nchw1024_r4_100603'

def setup_inputs(seed: int=0):
    np.random.seed(seed)
    _w = jnp.asarray

    def _rec_inputs():
        import jax
        import jax.numpy as jnp
        _gk = jax.random.key(seed)
        x = -0.0002928 + 1 * jax.random.normal(jax.random.fold_in(_gk, 1), (1, 256, 16, 16), jnp.float32)
        return x
    x = _rec_inputs()

    def _L0_conv_setup():
        import jax, jax.numpy as jnp
        import numpy as np
        EPS = 1e-05

        def _layernorm2d(x, w, b):
            mean = jnp.mean(x, axis=(-2, -1), keepdims=True)
            var = jnp.mean(jnp.square(x - mean), axis=(-2, -1), keepdims=True)
            return (x - mean) / jnp.sqrt(var + EPS) * w + b
        key = jax.random.key(seed)
        ks = jax.random.split(key, 6)
        b, seq, d = (1, 256, 16)
        x = jax.random.normal(ks[0], (b, seq, d, d), dtype=jnp.float32)
        log_A = jax.random.normal(ks[1], (d,), dtype=jnp.float32) * 0.02
        dt_w = jax.random.normal(ks[2], (1, d), dtype=jnp.float32) / np.sqrt(d)
        dt_b = jax.random.normal(ks[3], (1,), dtype=jnp.float32) * 0.01
        ln_w = jnp.ones((d, d), dtype=jnp.float32)
        ln_b = jnp.zeros((d, d), dtype=jnp.float32)
        return {'x': x, 'log_A': log_A, 'dt_w': dt_w, 'dt_b': dt_b, 'ln_w': ln_w, 'ln_b': ln_b}
    _L0_conv_all = _L0_conv_setup()
    _L0_conv_in = {k: v for k, v in _L0_conv_all.items() if k in ('log_A', 'dt_w', 'dt_b', 'ln_w', 'ln_b')}
    del _L0_conv_all

    def _L0_ffn_setup():
        import jax, jax.numpy as jnp
        import numpy as np
        key = jax.random.key(seed)
        k1, k2, k3 = jax.random.split(key, 3)
        B, S, D, E, H = (4, 512, 256, 8, 256)
        x = jax.random.normal(k1, (B, S, D), dtype=jnp.float32)
        Wg = jax.random.normal(k2, (D, E), dtype=jnp.float32) / np.sqrt(D)
        We = jax.random.normal(k3, (E, D, H), dtype=jnp.float32) / np.sqrt(D)
        be = jnp.zeros((E, H), dtype=jnp.float32)
        return {'x': x, 'Wg': Wg, 'We': We, 'be': be}
    _L0_ffn_all = _L0_ffn_setup()
    _L0_ffn_in = {k: v for k, v in _L0_ffn_all.items() if k in ('Wg', 'We', 'be')}
    del _L0_ffn_all
    return {'x': x, 'L0_conv_log_A': _L0_conv_in['log_A'], 'L0_conv_dt_w': _L0_conv_in['dt_w'], 'L0_conv_dt_b': _L0_conv_in['dt_b'], 'L0_conv_ln_w': _L0_conv_in['ln_w'], 'L0_conv_ln_b': _L0_conv_in['ln_b'], 'L0_ffn_Wg': _L0_ffn_in['Wg'], 'L0_ffn_We': _L0_ffn_in['We'], 'L0_ffn_be': _L0_ffn_in['be']}

def reference(x, L0_conv_log_A, L0_conv_dt_w, L0_conv_dt_b, L0_conv_ln_w, L0_conv_ln_b, L0_ffn_Wg, L0_ffn_We, L0_ffn_be):
    import jax
    import jax.numpy as jnp

    def _L0_conv_ref(x, log_A, dt_w, dt_b, ln_w, ln_b):
        import jax, jax.numpy as jnp
        import numpy as np
        EPS = 1e-05

        def _layernorm2d(x, w, b):
            mean = jnp.mean(x, axis=(-2, -1), keepdims=True)
            var = jnp.mean(jnp.square(x - mean), axis=(-2, -1), keepdims=True)
            return (x - mean) / jnp.sqrt(var + EPS) * w + b
        x_norm = _layernorm2d(x, ln_w, ln_b)
        b, seq, d, _ = x_norm.shape
        A_cont = -jnp.exp(log_A)
        dt = jax.nn.softplus(jnp.einsum('bsdc,c->bsd', x_norm, dt_w[0]) + dt_b[0])
        log_a = dt * A_cont
        cums = jnp.cumsum(log_a, axis=1)
        log_M = cums[:, :, None, :] - cums[:, None, :, :]
        idx = jnp.arange(seq)
        mask = idx[:, None] >= idx[None, :]
        log_M = jnp.where(mask[None, :, :, None], log_M, -jnp.inf)
        M = jnp.exp(log_M)
        out = jnp.einsum('btjr,bjrc->btrc', M, x_norm)
        return out

    def _L0_ffn_ref(x, Wg, We, be):
        import jax, jax.numpy as jnp
        import numpy as np
        B, S, D = x.shape
        E = Wg.shape[1]
        T = B * S
        xf = x.reshape(T, D)
        gates = jax.nn.softmax(xf @ Wg, axis=-1)
        top_g, top_i = jax.lax.top_k(gates, 2)
        top_g = top_g / jnp.sum(top_g, axis=-1, keepdims=True)
        tok = jnp.arange(T)
        dispatch = jnp.zeros((E, T), dtype=gates.dtype)
        for i in range(2):
            dispatch = dispatch.at[top_i[:, i], tok].add(top_g[:, i])
        y = jnp.einsum('td,edh->eth', xf, We) + be[:, None, :]
        out = jnp.einsum('et,eth->th', dispatch, y)
        return out.reshape(B, S, -1)

    def _gn(v, G=32, eps=1e-05):
        B_, C_, H_, W_ = v.shape
        g = v.reshape(B_, G, C_ // G, H_, W_)
        m = jnp.mean(g, axis=(2, 3, 4), keepdims=True)
        s = jnp.var(g, axis=(2, 3, 4), keepdims=True)
        return ((g - m) / jnp.sqrt(s + eps)).reshape(v.shape)

    def _ln_c(v, eps=1e-06):
        m = jnp.mean(v, axis=1, keepdims=True)
        s = jnp.var(v, axis=1, keepdims=True)
        return (v - m) / jnp.sqrt(s + eps)

    def _ln_t(v, eps=1e-05):
        m = jnp.mean(v, axis=-1, keepdims=True)
        s = jnp.var(v, axis=-1, keepdims=True)
        return (v - m) / jnp.sqrt(s + eps)

    def _to_tokens(v):
        B_, C_, H_, W_ = v.shape
        return v.reshape(B_, C_, H_ * W_).transpose(0, 2, 1)

    def _from_tokens(t, like):
        B_, C_, H_, W_ = like.shape
        return t.transpose(0, 2, 1).reshape(B_, C_, H_, W_)
    x = x + _L0_conv_ref(_ln_c(x), L0_conv_log_A, L0_conv_dt_w, L0_conv_dt_b, L0_conv_ln_w, L0_conv_ln_b)
    t = _to_tokens(x)
    t = t + _L0_ffn_ref(_ln_t(t), L0_ffn_Wg, L0_ffn_We, L0_ffn_be)
    x = _from_tokens(t, x)
    return x

_drawn_inputs = setup_inputs


def setup_inputs(seed=0):
    import zlib

    import numpy as np

    out = dict(_drawn_inputs(seed))
    spreads = {'L0_conv_ln_w': (1.0, 0.2), 'L0_conv_ln_b': (0.0, 0.1), 'L0_ffn_be': (0.0, 0.1)}
    factors = {'L0_conv_log_A': 4.003}
    for name, (base, spread) in spreads.items():
        noise = np.random.default_rng([zlib.crc32(name.encode()), seed]).standard_normal(out[name].shape)
        drawn = base * np.exp(spread * noise) if base else spread * noise
        out[name] = jnp.asarray(drawn.astype(out[name].dtype))
    for name, factor in factors.items():
        out[name] = (out[name] * factor).astype(out[name].dtype)
    return out
```

```python
from contextlib import ExitStack

import concourse.bass as bass
from concourse import mybir

F32 = mybir.dt.float32
U32 = mybir.dt.uint32
ALU = mybir.AluOpType
ACT = mybir.ActivationFunctionType

P = 128
EPS_CHANNEL = 1e-6
EPS_SPATIAL = 1e-5
EPS_TOKEN = 1e-5


def metaformer_block(nc, x, log_A, dt_w, dt_b, ln_w, ln_b, Wg, We, be, out):
    _, C, R, _ = x.shape
    T = R * R
    NT = T // P
    NC = C // P
    ROWS = P // R
    E, D, H = We.shape
    PAIR = 2
    NPAIR = E // PAIR
    assert T == NT * P and C == NC * P == D == H and PAIR * H == 512 and E == 8 and NC == 2

    x_dram = x.rearrange("b (c p) h w -> p (b c) (h w)", p=P)
    out_dram = out.rearrange("b (c p) h w -> p (b c) (h w)", p=P)

    with ExitStack() as ctx:
        def sb(name, shape, dt=F32):
            return ctx.enter_context(nc.sbuf_tensor(name, shape, dt))

        def bank(name):
            return ctx.enter_context(nc.psum_tensor(name, [P, 512], F32))

        def sem(name):
            return ctx.enter_context(nc.semaphore(name))

        x_ch = sb("x_ch", [P, NC, T])
        w_col = sb("w_col", [P, NT])
        b_col = sb("b_col", [P, NT])
        dtw_col = sb("dtw_col", [P, 1])
        dtb = sb("dtb", [P, 1])
        logA_row = sb("logA_row", [P, R])
        Wg_sb = sb("Wg_sb", [P, NC, E])
        be_sb = sb("be_sb", [E, H])
        We_sb = sb("We_sb", [P, NC, E, H])
        ident = sb("ident", [P, P])
        ones = sb("ones", [P, P])
        eps_channel = sb("eps_channel", [P, 1])
        eps_spatial = sb("eps_spatial", [P, 1])
        eps_token = sb("eps_token", [P, 1])
        one_col = sb("one_col", [P, 1])
        expert_id = sb("expert_id", [P, E])
        row_mask = sb("row_mask", [P, ROWS])
        A_row = sb("A_row", [P, R])
        wd_col = sb("wd_col", [P, 2, NT])
        proj = sb("proj", [P, NT, 2, ROWS])
        row_sums = sb("row_sums", [P, NT, 2, ROWS])
        stats_c = sb("stats_c", [P, NT, 6])
        mv_c = sb("mv_c", [P, NT, 2])
        lnv_c = sb("lnv_c", [P, NT])
        rstd_c = sb("rstd_c", [P, NT])
        xn = sb("xn", [P, NT, C])
        stats_s = sb("stats_s", [P, NC, 6])
        mv_s = sb("mv_s", [P, NC, 2])
        lnv_s = sb("lnv_s", [P, NC])
        rstd_s = sb("rstd_s", [P, NC])
        q = sb("q", [P, NC, T])
        x_norm = sb("x_norm", [P, NT, C])
        neg_g = sb("neg_g", [P, NC, R])
        neg_z = sb("neg_z", [P, NC, R])
        neg_abs_z = sb("neg_abs_z", [P, NC, R])
        exp_abs = sb("exp_abs", [P, NC, R])
        log1p = sb("log1p", [P, NC, R])
        neg_dt = sb("neg_dt", [P, NC, R])
        log_a = sb("log_a", [P, NC, R])
        decay = sb("decay", [P, NT, NC, P])
        y = sb("y", [P, NT, C])
        x1 = sb("x1", [P, NT, C])
        stats_t = sb("stats_t", [P, NT, 6])
        mv_t = sb("mv_t", [P, NT, 2])
        lnv_t = sb("lnv_t", [P, NT])
        rstd_t = sb("rstd_t", [P, NT])
        xc = sb("xc", [P, NT, C])
        xcT = sb("xcT", [P, NT, NC, P])
        logits = sb("logits", [P, NT, E])
        top = sb("top", [P, NT, E])
        top_id = sb("top_id", [P, NT, E], U32)
        top_idf = sb("top_idf", [P, NT, 2])
        gap = sb("gap", [P, NT])
        e2 = sb("e2", [P, NT])
        den = sb("den", [P, NT])
        g1 = sb("g1", [P, NT])
        g2 = sb("g2", [P, NT])
        first = sb("first", [P, NT, E])
        second = sb("second", [P, NT, E])
        gate = sb("gate", [P, NT, E])
        gate_rstd = sb("gate_rstd", [P, NT, E])
        gateT = sb("gateT", [E, NT, P])
        acc = sb("acc", [P, NT, E + 1, H])
        out_sb = sb("out_sb", [P, NC, T])

        B = [bank(f"bank{i}") for i in range(8)]
        xT_ps = [B[0], B[1]]
        xnT_ps = [B[2], B[3]]
        proj_ps = B[4]
        qT_ps = [B[5], B[6]]
        decay_ps = [B[2], B[3]]
        xcT_ps = [B[5], B[6]]
        gate_ps = [B[4], B[7]]
        y_ps = [B[0], B[1], B[2], B[3]]
        outT_ps = [B[5], B[6]]

        x_in = [sem(f"x_in{c}") for c in range(NC)]
        norm_in = sem("norm_in")
        logA_in = sem("logA_in")
        gate_in = sem("gate_in")
        We_in = [sem(f"We_in{p}") for p in range(NPAIR)]
        out_done = sem("out_done")

        ident_set = sem("ident_set")
        mask_set = sem("mask_set")
        expert_id_set = sem("expert_id_set")
        const_set = sem("const_set")
        A_set = sem("A_set")
        wd_set = sem("wd_set")
        proj_set = sem("proj_set")
        sums_ps_set = sem("sums_ps_set")
        row_sums_set = sem("row_sums_set")

        xT_ready = sem("xT_ready")
        stats_c_set = sem("stats_c_set")
        mv_c_set = sem("mv_c_set")
        lnv_c_set = sem("lnv_c_set")
        rstd_c_set = sem("rstd_c_set")
        xn_set = sem("xn_set")
        xnT_ready = sem("xnT_ready")
        G_ready = sem("G_ready")
        stats_s_set = sem("stats_s_set")
        mv_s_set = sem("mv_s_set")
        lnv_s_set = sem("lnv_s_set")
        rstd_s_set = sem("rstd_s_set")
        q_set = sem("q_set")
        qT_ready = sem("qT_ready")
        x_norm_set = sem("x_norm_set")
        neg_g_set = sem("neg_g_set")
        neg_z_set = sem("neg_z_set")
        neg_abs_z_set = sem("neg_abs_z_set")
        exp_abs_set = sem("exp_abs_set")
        log1p_set = sem("log1p_set")
        neg_dt_set = sem("neg_dt_set")
        log_a_set = sem("log_a_set")
        decay_set = sem("decay_set")
        decay_ready = sem("decay_ready")
        y_set = sem("y_set")
        x1_set = sem("x1_set")
        stats_t_set = sem("stats_t_set")
        mv_t_set = sem("mv_t_set")
        lnv_t_set = sem("lnv_t_set")
        rstd_t_set = sem("rstd_t_set")
        xc_set = sem("xc_set")
        xcT_ready = sem("xcT_ready")
        xcT_set = sem("xcT_set")
        logits_ready = sem("logits_ready")
        logits_set = sem("logits_set")
        top_set = sem("top_set")
        top_id_set = sem("top_id_set")
        top_idf_set = sem("top_idf_set")
        gap_set = sem("gap_set")
        e2_set = sem("e2_set")
        den_set = sem("den_set")
        g1_set = sem("g1_set")
        g2_set = sem("g2_set")
        pick_set = sem("pick_set")
        gate_set = sem("gate_set")
        gate_rstd_set = sem("gate_rstd_set")
        gateT_ready = sem("gateT_ready")
        gateT_set = sem("gateT_set")
        bias_ready = sem("bias_ready")
        y_ready = sem("y_ready")
        acc_set = sem("acc_set")
        outT_ready = sem("outT_ready")
        out_set = sem("out_set")

        block = ctx.enter_context(nc.Block())

        @block.sync
        def _(sp):
            sp.dma_start(x_ch[:, 0, :], x_dram[:, 0, :]).then_inc(x_in[0], 16)
            for col, ln in ((w_col, ln_w), (b_col, ln_b)):
                for t in range(NT):
                    rows = ln[t * ROWS:(t + 1) * ROWS, :]
                    sp.dma_start(col[:, t:t + 1], rows.rearrange("r (c a) -> (r c) a", a=1)).then_inc(norm_in, 16)
            for p in range(NPAIR):
                pair = slice(p * PAIR, (p + 1) * PAIR)
                for c in range(NC):
                    sp.dma_start(We_sb[:, c, pair, :],
                                 We[pair, c * P:(c + 1) * P, :].rearrange("e d h -> d e h")
                                 ).then_inc(We_in[p], 16)
            for t in range(NT):
                sp.wait_ge(out_set, t + 1)
                tokens = slice(t * P, (t + 1) * P)
                sp.dma_start(out_dram[:, :, tokens], out_sb[:, :, tokens]).then_inc(out_done, 16)
            sp.wait_ge(out_done, 16 * NT)

        @block.gpsimd
        def _(pool):
            nc.gpsimd.memset(ident[:], 0.0).then_inc(ident_set, 1)
            pool.wait_ge(ident_set, 1)
            nc.gpsimd.affine_select(out=ident[:], in_=ident[:], compare_op=ALU.not_equal, fill=1.0,
                                    base=0, pattern=[[-1, P]], channel_multiplier=1).then_inc(ident_set, 1)
            nc.gpsimd.memset(row_mask[:], 1.0).then_inc(mask_set, 1)
            pool.wait_ge(mask_set, 1)
            nc.gpsimd.affine_select(out=row_mask[:], in_=row_mask[:], compare_op=ALU.is_ge, fill=0.0,
                                    base=0, pattern=[[-R, ROWS]], channel_multiplier=1).then_inc(mask_set, 1)
            pool.wait_ge(mask_set, 2)
            nc.gpsimd.affine_select(out=row_mask[:], in_=row_mask[:], compare_op=ALU.is_ge, fill=0.0,
                                    base=R - 1, pattern=[[R, ROWS]], channel_multiplier=-1).then_inc(mask_set, 1)
            nc.gpsimd.iota(expert_id[:], pattern=[[1, E]], base=0, channel_multiplier=0,
                           allow_small_or_imprecise_dtypes=True).then_inc(expert_id_set, 1)

        @block.tensor
        def _(pe):
            def transpose(dst, src):
                return pe.transpose(dst, src, ident[:])

            pe.wait_ge(ident_set, 2)
            for c in range(NC):
                pe.wait_ge(x_in[c], 16)
            for t in range(NT):
                for c in range(NC):
                    mm = transpose(xT_ps[t][:, c * P:(c + 1) * P], x_ch[:, c, t * P:(t + 1) * P])
                mm.then_inc(xT_ready, 1)
            pe.wait_ge(const_set, 1)
            pe.wait_ge(proj_set, 2 * NT)
            for t in range(NT):
                mm = pe.matmul(proj_ps[:, t * 2 * ROWS:(t + 1) * 2 * ROWS], ones[:],
                               proj[:, t, :, :].rearrange("p k r -> p (k r)"), start=True, stop=True)
            mm.then_inc(sums_ps_set, 1)
            for t in range(NT):
                pe.wait_ge(xn_set, t + 1)
                for c in range(NC):
                    mm = transpose(xnT_ps[c][:, t * P:(t + 1) * P], xn[:, t, c * P:(c + 1) * P])
                    if t == NT - 1:
                        mm.then_inc(xnT_ready, 1)
            pe.wait_ge(row_sums_set, 1)
            for c in range(NC):
                for t in range(NT):
                    at = (c * NT + t) * ROWS
                    mm = pe.matmul(proj_ps[:, at:at + ROWS], xn[:, t, c * P:(c + 1) * P],
                                   proj[:, t, 0, :], start=True, stop=True)
            mm.then_inc(G_ready, 1)
            for t in range(NT):
                for c in range(NC):
                    pe.wait_ge(q_set, c + 1)
                    mm = transpose(qT_ps[t][:, c * P:(c + 1) * P], q[:, c, t * P:(t + 1) * P])
                mm.then_inc(qT_ready, 1)
            for t in range(NT):
                pe.wait_ge(decay_set, t + 1)
                for c in range(NC):
                    mm = transpose(decay_ps[t][:, c * P:(c + 1) * P], decay[:, t, c, :])
                mm.then_inc(decay_ready, 1)

            def center_transposes(t):
                pe.wait_ge(xc_set, t + 1)
                for c in range(NC):
                    mm = transpose(xcT_ps[t][:, c * P:(c + 1) * P], xc[:, t, c * P:(c + 1) * P])
                mm.then_inc(xcT_ready, 1)

            def expert_pair(t, p):
                n = t * NPAIR + p
                pe.wait_ge(We_in[p], 16 * NC)
                if n >= len(y_ps):
                    pe.wait_ge(acc_set, PAIR * (n - len(y_ps) + 1) + (n - len(y_ps)) // NPAIR + 1)
                for c in range(NC):
                    mm = pe.matmul(y_ps[n % len(y_ps)][:], xcT[:, t, c, :],
                                   We_sb[:, c, p * PAIR:(p + 1) * PAIR, :].rearrange("p e h -> p (e h)"),
                                   start=(c == 0), stop=(c == NC - 1))
                mm.then_inc(y_ready, 1)

            def gate_logits(t):
                pe.wait_ge(gate_in, 32)
                pe.wait_ge(xcT_set, t + 1)
                for c in range(NC):
                    mm = pe.matmul(gate_ps[t][:, 0:E], xcT[:, t, c, :], Wg_sb[:, c, :],
                                   start=(c == 0), stop=(c == NC - 1))
                mm.then_inc(logits_ready, 1)

            def gate_transpose(t):
                pe.wait_ge(gate_set, t + 1)
                transpose(gate_ps[t][0:E, 0:P], gate[:, t, :]).then_inc(gateT_ready, 1)

            def gate_bias(t):
                pe.wait_ge(gateT_set, t + 1)
                pe.matmul(gate_ps[t][:, 0:H], gateT[:, t, :], be_sb[:], start=True,
                          stop=True).then_inc(bias_ready, 1)

            def out_transposes(t):
                pe.wait_ge(acc_set, (t + 1) * (E + 1))
                for h in range(H // P):
                    mm = transpose(outT_ps[t][:, h * P:(h + 1) * P], acc[:, t, E, h * P:(h + 1) * P])
                mm.then_inc(outT_ready, 1)

            center_transposes(0)
            gate_logits(0)
            pe.wait_ge(x1_set, NT)
            expert_pair(0, 0)
            expert_pair(0, 1)
            gate_transpose(0)
            gate_bias(0)
            expert_pair(0, 2)
            center_transposes(1)
            expert_pair(0, 3)
            gate_logits(1)
            expert_pair(1, 0)
            expert_pair(1, 1)
            gate_transpose(1)
            gate_bias(1)
            expert_pair(1, 2)
            out_transposes(0)
            expert_pair(1, 3)
            out_transposes(1)

        @block.scalar
        def _(act):
            act.dma_start(x_ch[:, 1, :], x_dram[:, 1, :]).then_inc(x_in[1], 16)
            act.dma_start(dtw_col[:], dt_w.rearrange("a c -> c a").unsqueeze(0).broadcast_to([ROWS, R, 1])
                          ).then_inc(norm_in, 16)
            act.dma_start(dtb[:], dt_b.unsqueeze(0).broadcast_to([P, 1])).then_inc(norm_in, 16)
            act.dma_start(logA_row[:], log_A.unsqueeze(0).broadcast_to([P, R])).then_inc(logA_in, 16)
            act.dma_start(Wg_sb[:], Wg.rearrange("(c p) e -> p c e", p=P)).then_inc(gate_in, 16)
            act.dma_start(be_sb[:], be).then_inc(gate_in, 16)
            nc.scalar.preload_act_table_set("natural_log_exp_and_others")
            act.wait_ge(logA_in, 16)
            nc.scalar.activation(A_row[:], logA_row[:], ACT.Exp).then_inc(A_set, 1)
            act.wait_ge(const_set, 1)

            def rsqrt(rstd, lnv, var, eps, lnv_set, n, rstd_set):
                nc.scalar.activation(lnv, var, ACT.Ln, bias=eps[:]).then_inc(lnv_set, 1)
                act.wait_ge(lnv_set, n)
                nc.scalar.activation(rstd, lnv, ACT.Exp, scale=-0.5).then_inc(rstd_set, 1)

            for t in range(NT):
                act.wait_ge(mv_c_set, t + 1)
                rsqrt(rstd_c[:, t:t + 1], lnv_c[:, t:t + 1], mv_c[:, t, 1:2], eps_channel,
                      lnv_c_set, t + 1, rstd_c_set)
            for c in range(NC):
                act.wait_ge(mv_s_set, c + 1)
                rsqrt(rstd_s[:, c:c + 1], lnv_s[:, c:c + 1], mv_s[:, c, 1:2], eps_spatial,
                      lnv_s_set, c + 1, rstd_s_set)
            act.wait_ge(neg_abs_z_set, 1)
            nc.scalar.activation(exp_abs[:], neg_abs_z[:], ACT.Exp).then_inc(exp_abs_set, 1)
            act.wait_ge(exp_abs_set, 1)
            nc.scalar.activation(log1p[:], exp_abs[:], ACT.Ln, bias=one_col[:]).then_inc(log1p_set, 1)
            act.wait_ge(log_a_set, 1)
            for t in range(NT):
                rows = log_a[:, :, t * ROWS:(t + 1) * ROWS]
                nc.scalar.activation(decay[:, t, :, :].rearrange("p c (r k) -> p c r k", k=R),
                                     rows.unsqueeze(3).broadcast_to([P, NC, ROWS, R]),
                                     ACT.Exp).then_inc(decay_set, 1)

            def center(t):
                act.wait_ge(xcT_ready, t + 1)
                nc.scalar.copy(xcT[:, t, :, :].rearrange("p c t -> p (c t)"),
                               xcT_ps[t][:, 0:C]).then_inc(xcT_set, 1)

            def gates(t):
                act.wait_ge(mv_t_set, t + 1)
                rsqrt(rstd_t[:, t:t + 1], lnv_t[:, t:t + 1], mv_t[:, t, 1:2], eps_token,
                      lnv_t_set, t + 1, rstd_t_set)
                act.wait_ge(gap_set, t + 1)
                act.wait_ge(rstd_t_set, t + 1)
                nc.scalar.activation(e2[:, t:t + 1], gap[:, t:t + 1], ACT.Exp,
                                     scale=rstd_t[:, t:t + 1]).then_inc(e2_set, 1)
                act.wait_ge(gateT_ready, t + 1)
                nc.scalar.copy(gateT[:, t, :], gate_ps[t][0:E, 0:P]).then_inc(gateT_set, 1)

            center(0)
            gates(0)
            center(1)
            gates(1)
            for t in range(NT):
                act.wait_ge(outT_ready, t + 1)
                nc.scalar.copy(out_sb[:, :, t * P:(t + 1) * P],
                               outT_ps[t][:, 0:H].rearrange("p (h t) -> p h t", t=P)).then_inc(out_set, 1)

        @block.vector
        def _(dve):
            nc.vector.memset(ones[:], 1.0)
            nc.vector.memset(eps_channel[:], EPS_CHANNEL)
            nc.vector.memset(eps_spatial[:], EPS_SPATIAL)
            nc.vector.memset(eps_token[:], EPS_TOKEN)
            nc.vector.memset(one_col[:], 1.0).then_inc(const_set, 1)
            dve.wait_ge(norm_in, 16 * (2 * NT + 2))
            for k, col in enumerate((w_col, b_col)):
                nc.vector.tensor_scalar(wd_col[:, k, :], col[:], dtw_col[:, 0:1], None,
                                        ALU.mult).then_inc(wd_set, 1)
            dve.wait_ge(mask_set, 3)
            dve.wait_ge(wd_set, 2)
            for t in range(NT):
                for k in range(2):
                    nc.vector.tensor_scalar(proj[:, t, k, :], row_mask[:], wd_col[:, k, t:t + 1], None,
                                            ALU.mult).then_inc(proj_set, 1)

            for t in range(NT):
                dve.wait_ge(xT_ready, t + 1)
                nc.vector.bn_stats(stats_c[:, t, :], xT_ps[t][:, 0:C]).then_inc(stats_c_set, 1)
                dve.wait_ge(stats_c_set, t + 1)
                nc.vector.bn_aggr(mv_c[:, t, :], stats_c[:, t, :]).then_inc(mv_c_set, 1)
            dve.wait_ge(sums_ps_set, 1)
            sums = proj_ps[:, 0:NT * 2 * ROWS].rearrange("p (t k r) -> p t k r", t=NT, k=2)
            nc.vector.tensor_copy(row_sums[:, :, 0, :], sums[:, :, 0, :])
            nc.vector.tensor_scalar(row_sums[:, :, 1, :], sums[:, :, 1, :], dtb[:, 0:1], None,
                                    ALU.add).then_inc(row_sums_set, 1)
            for t in range(NT):
                dve.wait_ge(mv_c_set, t + 1)
                dve.wait_ge(rstd_c_set, t + 1)
                nc.vector.tensor_scalar(xn[:, t, :], xT_ps[t][:, 0:C], mv_c[:, t, 0:1], rstd_c[:, t:t + 1],
                                        ALU.subtract, ALU.mult).then_inc(xn_set, 1)

            for c in range(NC):
                dve.wait_ge(xnT_ready, c + 1)
                nc.vector.bn_stats(stats_s[:, c, :], xnT_ps[c][:, 0:T]).then_inc(stats_s_set, 1)
                dve.wait_ge(stats_s_set, c + 1)
                nc.vector.bn_aggr(mv_s[:, c, :], stats_s[:, c, :]).then_inc(mv_s_set, 1)
            dve.wait_ge(mv_s_set, NC)
            for c in range(NC):
                dve.wait_ge(rstd_s_set, c + 1)
                nc.vector.tensor_scalar(q[:, c, :], xnT_ps[c][:, 0:T], mv_s[:, c, 0:1], rstd_s[:, c:c + 1],
                                        ALU.subtract, ALU.mult).then_inc(q_set, 1)

            dve.wait_ge(row_sums_set, 1)
            dve.wait_ge(G_ready, 1)
            G = proj_ps[:, 0:NC * R].rearrange("p (c t r) -> p c t r", c=NC, t=NT)
            for c in range(NC):
                nc.vector.scalar_tensor_tensor(
                    out=neg_g[:, c, :].rearrange("p (t r) -> p t r", t=NT), in0=row_sums[:, :, 0, :],
                    scalar=mv_s[:, c, 0:1], in1=G[:, c, :, :],
                    op0=ALU.mult, op1=ALU.subtract).then_inc(neg_g_set, 1)
            for c in range(NC):
                dve.wait_ge(neg_g_set, c + 1)
                nc.vector.scalar_tensor_tensor(
                    out=neg_z[:, c, :].rearrange("p (t r) -> p t r", t=NT),
                    in0=neg_g[:, c, :].rearrange("p (t r) -> p t r", t=NT),
                    scalar=rstd_s[:, c:c + 1], in1=row_sums[:, :, 1, :],
                    op0=ALU.mult, op1=ALU.subtract).then_inc(neg_z_set, 1)
            dve.wait_ge(neg_z_set, NC)
            nc.vector.scalar_tensor_tensor(out=neg_abs_z[:], in0=neg_z[:], scalar=-1.0, in1=neg_z[:],
                                           op0=ALU.mult, op1=ALU.min).then_inc(neg_abs_z_set, 1)

            def scale_shift(t):
                dve.wait_ge(qT_ready, t + 1)
                nc.vector.tensor_scalar(x_norm[:, t, :], qT_ps[t][:, 0:C], w_col[:, t:t + 1],
                                        b_col[:, t:t + 1], ALU.mult, ALU.add).then_inc(x_norm_set, 1)

            scale_shift(0)
            dve.wait_ge(log1p_set, 1)
            nc.vector.scalar_tensor_tensor(out=neg_dt[:], in0=neg_z[:], scalar=0.0, in1=log1p[:],
                                           op0=ALU.min, op1=ALU.subtract).then_inc(neg_dt_set, 1)
            dve.wait_ge(neg_dt_set, 1)
            dve.wait_ge(A_set, 1)
            nc.vector.tensor_tensor(log_a[:], neg_dt[:], A_row[:].unsqueeze(1).broadcast_to([P, NC, R]),
                                    ALU.mult).then_inc(log_a_set, 1)
            scale_shift(1)

            for t in range(NT):
                dve.wait_ge(decay_ready, t + 1)
                dve.wait_ge(x_norm_set, t + 1)
                nc.vector.tensor_tensor_scan(y[:, t, :], decay_ps[t][:, 0:C], x_norm[:, t, :], 0.0,
                                             ALU.mult, ALU.add).then_inc(y_set, 1)
                dve.wait_ge(y_set, t + 1)
                nc.vector.tensor_tensor(x1[:, t, :], y[:, t, :], xT_ps[t][:, 0:C],
                                        ALU.add).then_inc(x1_set, 1)
                dve.wait_ge(x1_set, t + 1)
                nc.vector.bn_stats(stats_t[:, t, :], x1[:, t, :]).then_inc(stats_t_set, 1)
                dve.wait_ge(stats_t_set, t + 1)
                nc.vector.bn_aggr(mv_t[:, t, :], stats_t[:, t, :]).then_inc(mv_t_set, 1)
                dve.wait_ge(mv_t_set, t + 1)
                nc.vector.tensor_scalar(xc[:, t, :], x1[:, t, :], mv_t[:, t, 0:1], None,
                                        ALU.subtract).then_inc(xc_set, 1)

            def gates(t):
                dve.wait_ge(logits_ready, t + 1)
                nc.vector.tensor_copy(logits[:, t, :], gate_ps[t][:, 0:E]).then_inc(logits_set, 1)
                dve.wait_ge(logits_set, t + 1)
                nc.vector.max(top[:, t, :], logits[:, t, :]).then_inc(top_set, 1)
                dve.wait_ge(top_set, t + 1)
                nc.vector.tensor_tensor(gap[:, t:t + 1], top[:, t, 1:2], top[:, t, 0:1],
                                        ALU.subtract).then_inc(gap_set, 1)
                nc.vector.max_index(top_id[:, t, :], top[:, t, :], logits[:, t, :]).then_inc(top_id_set, 1)
                dve.wait_ge(top_id_set, t + 1)
                nc.vector.tensor_copy(top_idf[:, t, :], top_id[:, t, 0:2]).then_inc(top_idf_set, 1)
                dve.wait_ge(e2_set, t + 1)
                nc.vector.tensor_scalar(den[:, t:t + 1], e2[:, t:t + 1], 1.0, None,
                                        ALU.add).then_inc(den_set, 1)
                dve.wait_ge(den_set, t + 1)
                nc.vector.reciprocal(g1[:, t:t + 1], den[:, t:t + 1]).then_inc(g1_set, 1)
                dve.wait_ge(g1_set, t + 1)
                nc.vector.tensor_tensor(g2[:, t:t + 1], e2[:, t:t + 1], g1[:, t:t + 1],
                                        ALU.mult).then_inc(g2_set, 1)
                dve.wait_ge(top_idf_set, t + 1)
                nc.vector.tensor_scalar(first[:, t, :], expert_id[:], top_idf[:, t, 0:1], g1[:, t:t + 1],
                                        ALU.is_equal, ALU.mult).then_inc(pick_set, 1)
                dve.wait_ge(g2_set, t + 1)
                nc.vector.tensor_scalar(second[:, t, :], expert_id[:], top_idf[:, t, 1:2], g2[:, t:t + 1],
                                        ALU.is_equal, ALU.mult).then_inc(pick_set, 1)
                dve.wait_ge(pick_set, 2 * (t + 1))
                nc.vector.tensor_tensor(gate[:, t, :], first[:, t, :], second[:, t, :],
                                        ALU.add).then_inc(gate_set, 1)
                dve.wait_ge(gate_set, t + 1)
                dve.wait_ge(rstd_t_set, t + 1)
                nc.vector.tensor_scalar(gate_rstd[:, t, :], gate[:, t, :], rstd_t[:, t:t + 1], None,
                                        ALU.mult).then_inc(gate_rstd_set, 1)

            def add_bias(t):
                dve.wait_ge(bias_ready, t + 1)
                nc.vector.tensor_tensor(acc[:, t, 0, :], x1[:, t, :], gate_ps[t][:, 0:H],
                                        ALU.add).then_inc(acc_set, 1)

            def add_expert(t, e):
                n = t * NPAIR + e // PAIR
                at = (e % PAIR) * H
                dve.wait_ge(gate_rstd_set, t + 1)
                dve.wait_ge(y_ready, n + 1)
                dve.wait_ge(acc_set, t * (E + 1) + e + 1)
                nc.vector.scalar_tensor_tensor(
                    out=acc[:, t, e + 1, :], in0=y_ps[n % len(y_ps)][:, at:at + H],
                    scalar=gate_rstd[:, t, e:e + 1], in1=acc[:, t, e, :],
                    op0=ALU.mult, op1=ALU.add).then_inc(acc_set, 1)

            dve.wait_ge(expert_id_set, 1)
            gates(0)
            add_bias(0)
            for e in range(E):
                add_expert(0, e)
            gates(1)
            add_bias(1)
            for e in range(E):
                add_expert(1, e)


_INS = {"x": "x", "L0_conv_log_A": "log_A", "L0_conv_dt_w": "dt_w", "L0_conv_dt_b": "dt_b",
        "L0_conv_ln_w": "ln_w", "L0_conv_ln_b": "ln_b", "L0_ffn_Wg": "Wg", "L0_ffn_We": "We",
        "L0_ffn_be": "be"}


def kernel(**inputs):
    import numpy as np
    import concourse.bacc as bacc
    from concourse.bass_utils import run_bass_kernel_spmd

    nc = bacc.Bacc("TRN2", target_bir_lowering=False, num_devices=1)
    arrays, args = {}, {}
    for name, arg in _INS.items():
        a = np.ascontiguousarray(inputs[name])
        arrays[f"in_{name}"] = a
        args[arg] = nc.dram_tensor(f"in_{name}", a.shape, mybir.dt.from_np(a.dtype),
                                   kind="ExternalInput").ap()
    args["out"] = nc.dram_tensor("out_x", arrays["in_x"].shape, F32, kind="ExternalOutput").ap()
    metaformer_block(nc, **args)
    result = run_bass_kernel_spmd(nc, [arrays], core_ids=[0])
    return result.results[0]["out_x"]
```

```python
from contextlib import ExitStack

import concourse.bass as bass
from concourse import mybir

F32 = mybir.dt.float32
F32R = mybir.dt.float32r
BF16 = mybir.dt.bfloat16
U32 = mybir.dt.uint32
ALU = mybir.AluOpType
ACT = mybir.ActivationFunctionType

P = 128
EPS_CHANNEL = 1e-6
EPS_SPATIAL = 1e-5
EPS_TOKEN = 1e-5


def param_columns(C, R, E):
    NT, NC, ROWS = R * R // P, C // P, P // R
    at, start = {}, 0
    for name, width in (("ident", P), ("row_mask", ROWS), ("expert_id", E), ("ln", NT * 2), ("dt_w", 1),
                        ("dt_b", NT * 2 * ROWS), ("log_A", R), ("Wg", NC * E)):
        at[name] = slice(start, start + width)
        start += width
    return at, start


def metaformer_block(nc, x, params, We, be, out):
    T, C = x.shape
    E, D, H = be.shape[0], We.shape[0], be.shape[1]
    R = int(T ** 0.5)
    NT = T // P
    NC = C // P
    ROWS = P // R
    PAIR = 2
    NPAIR = E // PAIR
    assert R * R == T == NT * P and C == NC * P == D == H and PAIR * H == 512 and E == 8
    assert NC == 2 and NT == 2

    at, n_params = param_columns(C, R, E)
    x_dram = x.rearrange("(t p) c -> p t c", p=P)
    out_dram = out.rearrange("(t p) c -> p t c", p=P)
    We_dram = We.rearrange("(c p) (e h) -> p c e h", p=P, e=E)

    with ExitStack() as ctx:
        def sb(name, shape, dt=F32):
            return ctx.enter_context(nc.sbuf_tensor(name, shape, dt))

        def sem(name):
            return ctx.enter_context(nc.semaphore(name))

        x_tok = sb("x_tok", [P, NT, C])
        par = sb("par", [P, n_params])
        be_sb = sb("be_sb", [E, H])
        We_sb = sb("We_sb", [P, NC, E, H])
        ident = par[:, at["ident"]]
        row_mask = par[:, at["row_mask"]]
        expert_id = par[:, at["expert_id"]]
        ln_col = par[:, at["ln"]]
        dtw_col = par[:, at["dt_w"]]
        dtb_row = par[:, at["dt_b"]]
        logA_row = par[:, at["log_A"]]
        Wg_par = par[:, at["Wg"]].rearrange("p (c e) -> p c e", c=NC)
        ones = sb("ones", [P, P])
        warm = sb("warm", [P, 1], BF16)
        eps_channel = sb("eps_channel", [P, 1])
        eps_spatial = sb("eps_spatial", [P, 1])
        eps_token = sb("eps_token", [P, 1])
        one_col = sb("one_col", [P, 1])
        A_row = sb("A_row", [P, R])
        proj = sb("proj", [P, NT, 2, ROWS])
        row_sums = sb("row_sums", [P, NT, 2, ROWS])
        W_hi = sb("W_hi", [P, NPAIR, NC, PAIR * H], F32R)
        W_lo = sb("W_lo", [P, NPAIR, NC, PAIR * H], F32R)
        Wg_hi = sb("Wg_hi", [P, NC, E], F32R)
        Wg_lo = sb("Wg_lo", [P, NC, E], F32R)
        stats_c = sb("stats_c", [P, NT, 6])
        mv_c = sb("mv_c", [P, NT, 2])
        lnv_c = sb("lnv_c", [P, NT])
        rstd_c = sb("rstd_c", [P, NT])
        xn = sb("xn", [P, NT, C])
        stats_s = sb("stats_s", [P, NC, 6])
        mv_s = sb("mv_s", [P, NC, 2])
        lnv_s = sb("lnv_s", [P, NC])
        rstd_s = sb("rstd_s", [P, NC])
        shift_s = sb("shift_s", [P, 1])
        q = sb("q", [P, NC, T])
        x_norm = sb("x_norm", [P, NT, C])
        neg_g = sb("neg_g", [P, NC, R])
        neg_z = sb("neg_z", [P, NC, R])
        neg_abs_z = sb("neg_abs_z", [P, NC, R])
        exp_abs = sb("exp_abs", [P, NC, R])
        log1p = sb("log1p", [P, NC, R])
        neg_dt = sb("neg_dt", [P, NC, R])
        log_a = sb("log_a", [P, NC, R])
        decay = sb("decay", [P, NT, NC, P])
        y = sb("y", [P, NT, C])
        x1 = sb("x1", [P, NT, C])
        stats_t = sb("stats_t", [P, NT, 6])
        mv_t = sb("mv_t", [P, NT, 2])
        lnv_t = sb("lnv_t", [P, NT])
        rstd_t = sb("rstd_t", [P, NT])
        xc = sb("xc", [P, NT, C])
        xcT_hi = sb("xcT_hi", [P, NT, NC, P], F32R)
        xcT_lo = sb("xcT_lo", [P, NT, NC, P], F32R)
        top = sb("top", [P, NT, E])
        top_id = sb("top_id", [P, NT, E], U32)
        top_idf = sb("top_idf", [P, NT, 2])
        gap = sb("gap", [P, NT])
        e2 = sb("e2", [P, NT])
        den = sb("den", [P, NT])
        g1 = sb("g1", [P, NT])
        first = sb("first", [P, NT, E])
        second = sb("second", [P, NT, E])
        picks = sb("picks", [P, NT, E])
        gate = sb("gate", [P, NT, E])
        gate_rstd = sb("gate_rstd", [P, NT, E])
        gateT = sb("gateT", [E, NT, P])
        sum_even = sb("sum_even", [P, NT, H])
        sum_odd = sb("sum_odd", [P, NT, H])

        banks = [ctx.enter_context(nc.psum_tensor(f"bank{i}", [P, 512], F32)) for i in range(8)]
        xnT_ps = banks[0:2]
        decay_ps = banks[0:2]
        qT_ps = banks[2:4]
        xcT_ps = banks[2:4]
        proj_ps = banks[4]
        gate_ps = banks[4:6]
        warm_ps = banks[5]
        pair_banks = [banks[6], banks[7], banks[0], banks[1]]
        y_ps = [[pair_banks[e // PAIR][:, e % PAIR * H:(e % PAIR + 1) * H] for e in range(E)]
                for t in range(NT)]
        y_ps[NT - 1][E - 1] = banks[2][:, 0:H]

        x_in = [sem(f"x_in{t}") for t in range(NT)]
        par_in = sem("par_in")
        be_in = sem("be_in")
        We_in = [sem(f"We_in{p}") for p in range(NPAIR)]
        out_done = sem("out_done")

        const_set = sem("const_set")
        warm_set = sem("warm_set")
        A_set = sem("A_set")
        proj_set = sem("proj_set")
        sums_ready = sem("sums_ready")
        row_sums_set = sem("row_sums_set")
        W_hi_set = sem("W_hi_set")
        W_lo_set = sem("W_lo_set")
        Wg_hi_set = sem("Wg_hi_set")
        Wg_lo_set = sem("Wg_lo_set")

        stats_c_set = sem("stats_c_set")
        mv_c_set = sem("mv_c_set")
        lnv_c_set = sem("lnv_c_set")
        rstd_c_set = sem("rstd_c_set")
        xn_set = sem("xn_set")
        xnT_ready = sem("xnT_ready")
        G_ready = sem("G_ready")
        stats_s_set = sem("stats_s_set")
        mv_s_set = sem("mv_s_set")
        lnv_s_set = sem("lnv_s_set")
        rstd_s_set = sem("rstd_s_set")
        shift_s_set = sem("shift_s_set")
        q_set = [sem(f"q_set{c}") for c in range(NC)]
        qT_ready = sem("qT_ready")
        x_norm_set = sem("x_norm_set")
        neg_g_set = sem("neg_g_set")
        neg_z_set = sem("neg_z_set")
        neg_abs_z_set = sem("neg_abs_z_set")
        exp_abs_set = sem("exp_abs_set")
        log1p_set = sem("log1p_set")
        neg_dt_set = sem("neg_dt_set")
        log_a_set = sem("log_a_set")
        decay_set = sem("decay_set")
        decay_ready = sem("decay_ready")
        y_set = sem("y_set")
        x1_set = sem("x1_set")
        stats_t_set = sem("stats_t_set")
        mv_t_set = sem("mv_t_set")
        lnv_t_set = sem("lnv_t_set")
        rstd_t_set = sem("rstd_t_set")
        xc_set = sem("xc_set")
        xcT_ready = sem("xcT_ready")
        xcT_hi_set = sem("xcT_hi_set")
        xcT_lo_set = sem("xcT_lo_set")
        logits_ready = sem("logits_ready")
        top_set = sem("top_set")
        top_id_set = sem("top_id_set")
        top_idf_set = sem("top_idf_set")
        gap_set = sem("gap_set")
        e2_set = sem("e2_set")
        den_set = sem("den_set")
        g1_set = sem("g1_set")
        first_set = sem("first_set")
        second_set = sem("second_set")
        picks_set = sem("picks_set")
        gate_set = sem("gate_set")
        gate_rstd_set = sem("gate_rstd_set")
        gateT_ready = sem("gateT_ready")
        gateT_set = sem("gateT_set")
        bias_ready = sem("bias_ready")
        y_ready = [sem(f"y_ready{t}") for t in range(NT)]
        summed = [sem(f"summed{t}") for t in range(NT)]
        order = [0, 1, 2, 3, "bias", "join", 4, 5, 6, 7]
        step = {what: n + 1 for n, what in enumerate(order)}
        STEPS = len(order)

        block = ctx.enter_context(nc.Block())

        @block.sync
        def _(sp):
            for t in range(NT):
                sp.dma_start(x_tok[:, t, :], x_dram[:, t, :]).then_inc(x_in[t], 16)
            sp.dma_start(par[:], params).then_inc(par_in, 16)
            for p in range(NPAIR):
                pair = slice(p * PAIR, (p + 1) * PAIR)
                sp.dma_start(We_sb[:, :, pair, :].rearrange("p c e h -> p c (e h)"),
                             We_dram[:, :, pair, :].rearrange("p c e h -> p c (e h)")).then_inc(We_in[p], 16)
            sp.dma_start(be_sb[:], be).then_inc(be_in, 16)
            for t in range(NT):
                sp.wait_ge(summed[t], STEPS)
                sp.dma_start(out_dram[:, t, :], sum_even[:, t, :]).then_inc(out_done, 16)
            sp.wait_ge(out_done, 16 * NT)

        @block.gpsimd
        def _(pool):
            for p in range(NPAIR):
                if p == 1:
                    pool.wait_ge(log_a_set, 1)
                if p == 2:
                    pool.wait_ge(xc_set, 1)
                for c in range(NC):
                    pool.wait_ge(W_hi_set, p * NC + c + 1)
                    nc.gpsimd.tensor_tensor(W_lo[:, p, c, :],
                                            We_sb[:, c, p * PAIR:(p + 1) * PAIR, :].rearrange("p e h -> p (e h)"),
                                            W_hi[:, p, c, :], ALU.subtract).then_inc(W_lo_set, 1)

        @block.tensor
        def _(pe):
            def transpose(dst, src):
                return pe.transpose(dst, src, ident)

            def keep_warm(n):
                for _ in range(n):
                    pe.matmul(warm_ps[:], warm[:].broadcast_to([P, P]), warm[:].broadcast_to([P, 512]),
                              start=True, stop=True)

            pe.wait_ge(warm_set, 1)
            keep_warm(10)

            def xn_transposes(t):
                pe.wait_ge(xn_set, t + 1)
                for c in range(NC):
                    mm = transpose(xnT_ps[c][:, t * P:(t + 1) * P], xn[:, t, c * P:(c + 1) * P])
                    if t == NT - 1:
                        mm.then_inc(xnT_ready, 1)

            def project(c, t):
                at = (c * NT + t) * ROWS
                return pe.matmul(proj_ps[:, at:at + ROWS], xn[:, t, c * P:(c + 1) * P],
                                 proj[:, t, 0, :], start=True, stop=True)

            xn_transposes(0)
            pe.wait_ge(const_set, 1)
            pe.wait_ge(proj_set, 1)
            for t in range(NT):
                mm = pe.matmul(proj_ps[:, t * 2 * ROWS:(t + 1) * 2 * ROWS], ones[:],
                               proj[:, t, :, :].rearrange("p k r -> p (k r)"), start=True, stop=True)
            mm.then_inc(sums_ready, 1)
            xn_transposes(1)
            pe.wait_ge(row_sums_set, 1)
            for t in range(NT):
                for c in range(NC):
                    mm = project(c, t)
            mm.then_inc(G_ready, 1)
            keep_warm(6)
            for c in reversed(range(NC)):
                pe.wait_ge(q_set[c], 1)
                for t in range(NT):
                    mm = transpose(qT_ps[t][:, c * P:(c + 1) * P], q[:, c, t * P:(t + 1) * P])
                    if c == 0:
                        mm.then_inc(qT_ready, 1)
            for t in range(NT):
                pe.wait_ge(decay_set, t + 1)
                for c in range(NC):
                    mm = transpose(decay_ps[t][:, c * P:(c + 1) * P], decay[:, t, c, :])
                mm.then_inc(decay_ready, 1)
            keep_warm(7)

            def center_transposes(t):
                pe.wait_ge(xc_set, t + 1)
                for c in range(NC):
                    mm = transpose(xcT_ps[t][:, c * P:(c + 1) * P], xc[:, t, c * P:(c + 1) * P])
                mm.then_inc(xcT_ready, 1)

            def expert(t, p, experts):
                width = len(experts) * H
                e0 = experts[0]
                first_bank = y_ps[t][e0]
                dst = pair_banks[p][:, 0:width] if len(experts) == PAIR else first_bank
                cols = slice((e0 % PAIR) * H, (e0 % PAIR) * H + width)
                products = [(xcT_hi, W_hi), (xcT_hi, W_lo), (xcT_lo, W_hi)]
                for k, (left, right) in enumerate(products):
                    if right is W_hi:
                        pe.wait_ge(W_hi_set, (p + 1) * NC)
                    else:
                        pe.wait_ge(W_lo_set, (p + 1) * NC)
                    if left is xcT_hi:
                        pe.wait_ge(xcT_hi_set, t + 1)
                    else:
                        pe.wait_ge(xcT_lo_set, t + 1)
                    for c in range(NC):
                        mm = pe.matmul(dst, left[:, t, c, :], right[:, p, c, cols],
                                       start=(k == 0 and c == 0),
                                       stop=(k == len(products) - 1 and c == NC - 1))
                mm.then_inc(y_ready[t], len(experts))

            def gate_logits(t):
                pe.wait_ge(Wg_lo_set, 1)
                pe.wait_ge(xcT_lo_set, t + 1)
                products = [(xcT_hi, Wg_hi), (xcT_hi, Wg_lo), (xcT_lo, Wg_hi)]
                for k, (left, right) in enumerate(products):
                    for c in range(NC):
                        mm = pe.matmul(gate_ps[t][:, 0:E], left[:, t, c, :], right[:, c, :],
                                       start=(k == 0 and c == 0),
                                       stop=(k == len(products) - 1 and c == NC - 1))
                mm.then_inc(logits_ready, 1)

            def gate_transpose(t):
                pe.wait_ge(gate_set, t + 1)
                transpose(gate_ps[t][0:E, 0:P], gate[:, t, :]).then_inc(gateT_ready, 1)

            def gate_bias(t):
                pe.wait_ge(be_in, 16)
                pe.wait_ge(gateT_set, t + 1)
                pe.matmul(gate_ps[t][:, 0:H], gateT[:, t, :], be_sb[:], start=True,
                          stop=True).then_inc(bias_ready, 1)

            center_transposes(0)
            keep_warm(1)
            expert(0, 0, (0, 1))
            pe.wait_ge(x_norm_set, 2)
            center_transposes(1)
            gate_logits(0)
            expert(0, 1, (2, 3))
            gate_logits(1)
            pe.wait_ge(y_set, 2)
            expert(0, 2, (4, 5))
            expert(0, 3, (6, 7))
            gate_transpose(0)
            gate_bias(0)
            for p in range(NPAIR - 1):
                pe.wait_ge(summed[0], step[PAIR * p + 1])
                expert(1, p, (PAIR * p, PAIR * p + 1))
                if p == 0:
                    gate_transpose(1)
                    gate_bias(1)
            pe.wait_ge(summed[0], STEPS)
            expert(1, 3, (6,))
            expert(1, 3, (7,))

        @block.scalar
        def _(act):
            nc.scalar.preload_act_table_set("natural_log_exp_and_others")
            act.wait_ge(const_set, 1)
            def rsqrt(rstd, lnv, var, eps, lnv_set, n, rstd_set):
                nc.scalar.activation(lnv, var, ACT.Ln, bias=eps[:]).then_inc(lnv_set, 1)
                act.wait_ge(lnv_set, n)
                nc.scalar.activation(rstd, lnv, ACT.Exp, scale=-0.5).then_inc(rstd_set, 1)

            def round_W(p, c):
                act.wait_ge(We_in[p], 16)
                nc.scalar.copy(W_hi[:, p, c, :],
                               We_sb[:, c, p * PAIR:(p + 1) * PAIR, :].rearrange("p e h -> p (e h)")
                               ).then_inc(W_hi_set, 1)

            for t in range(NT):
                act.wait_ge(mv_c_set, t + 1)
                rsqrt(rstd_c[:, t:t + 1], lnv_c[:, t:t + 1], mv_c[:, t, 1:2], eps_channel,
                      lnv_c_set, t + 1, rstd_c_set)
            act.wait_ge(par_in, 16)
            nc.scalar.activation(A_row[:], logA_row, ACT.Exp).then_inc(A_set, 1)
            round_W(0, 0)
            round_W(0, 1)
            for c in range(NC):
                act.wait_ge(mv_s_set, c + 1)
                rsqrt(rstd_s[:, c:c + 1], lnv_s[:, c:c + 1], mv_s[:, c, 1:2], eps_spatial,
                      lnv_s_set, c + 1, rstd_s_set)
            act.wait_ge(shift_s_set, 1)
            nc.scalar.activation(q[:, NC - 1, :], xnT_ps[NC - 1][:, 0:T], ACT.Identity,
                                 bias=shift_s[:], scale=rstd_s[:, NC - 1:NC]).then_inc(q_set[NC - 1], 1)
            act.wait_ge(neg_abs_z_set, 1)
            nc.scalar.activation(exp_abs[:], neg_abs_z[:], ACT.Exp).then_inc(exp_abs_set, 1)
            act.wait_ge(exp_abs_set, 1)
            nc.scalar.activation(log1p[:], exp_abs[:], ACT.Ln, bias=one_col[:]).then_inc(log1p_set, 1)
            act.wait_ge(log_a_set, 1)
            for t in range(NT):
                rows = log_a[:, :, t * ROWS:(t + 1) * ROWS]
                nc.scalar.activation(decay[:, t, :, :].rearrange("p c (r k) -> p c r k", k=R),
                                     rows.unsqueeze(3).broadcast_to([P, NC, ROWS, R]),
                                     ACT.Exp).then_inc(decay_set, 1)
            round_W(1, 0)
            round_W(1, 1)
            round_W(2, 0)
            round_W(2, 1)

            def token_rsqrt(t):
                act.wait_ge(mv_t_set, t + 1)
                rsqrt(rstd_t[:, t:t + 1], lnv_t[:, t:t + 1], mv_t[:, t, 1:2], eps_token,
                      lnv_t_set, t + 1, rstd_t_set)

            def round_xcT(t):
                act.wait_ge(xcT_ready, t + 1)
                nc.scalar.copy(xcT_hi[:, t, :, :].rearrange("p c t -> p (c t)"),
                               xcT_ps[t][:, 0:C]).then_inc(xcT_hi_set, 1)

            def second_exp(t):
                act.wait_ge(gap_set, t + 1)
                act.wait_ge(rstd_t_set, t + 1)
                nc.scalar.activation(e2[:, t:t + 1], gap[:, t:t + 1], ACT.Exp,
                                     scale=rstd_t[:, t:t + 1]).then_inc(e2_set, 1)

            def copy_gateT(t):
                act.wait_ge(gateT_ready, t + 1)
                nc.scalar.copy(gateT[:, t, :], gate_ps[t][0:E, 0:P]).then_inc(gateT_set, 1)

            round_xcT(0)
            token_rsqrt(0)
            round_W(3, 0)
            round_W(3, 1)
            token_rsqrt(1)
            round_xcT(1)
            second_exp(0)
            second_exp(1)
            copy_gateT(0)
            copy_gateT(1)

        @block.vector
        def _(dve):
            nc.vector.memset(warm[:], 1.0).then_inc(warm_set, 1)
            nc.vector.memset(ones[:], 1.0)
            nc.vector.memset(eps_channel[:], EPS_CHANNEL)
            nc.vector.memset(eps_spatial[:], EPS_SPATIAL)
            nc.vector.memset(eps_token[:], EPS_TOKEN)
            nc.vector.memset(one_col[:], 1.0).then_inc(const_set, 1)

            def channel_stats(t):
                dve.wait_ge(x_in[t], 16)
                nc.vector.bn_stats(stats_c[:, t, :], x_tok[:, t, :]).then_inc(stats_c_set, 1)
                dve.wait_ge(stats_c_set, t + 1)
                nc.vector.bn_aggr(mv_c[:, t, :], stats_c[:, t, :]).then_inc(mv_c_set, 1)

            def channel_norm(t):
                dve.wait_ge(mv_c_set, t + 1)
                dve.wait_ge(rstd_c_set, t + 1)
                nc.vector.tensor_scalar(xn[:, t, :], x_tok[:, t, :], mv_c[:, t, 0:1], rstd_c[:, t:t + 1],
                                        ALU.subtract, ALU.mult).then_inc(xn_set, 1)

            channel_stats(0)
            channel_stats(1)
            dve.wait_ge(par_in, 16)
            nc.vector.scalar_tensor_tensor(
                out=proj[:].rearrange("p t k r -> p (t k) r"),
                in0=ln_col.unsqueeze(2).broadcast_to([P, NT * 2, ROWS]), scalar=dtw_col,
                in1=row_mask.unsqueeze(1).broadcast_to([P, NT * 2, ROWS]),
                op0=ALU.mult, op1=ALU.mult).then_inc(proj_set, 1)
            channel_norm(0)
            channel_norm(1)
            dve.wait_ge(sums_ready, 1)
            nc.vector.tensor_tensor(row_sums[:].rearrange("p t k r -> p (t k r)"), dtb_row,
                                    proj_ps[:, 0:NT * 2 * ROWS], ALU.add).then_inc(row_sums_set, 1)
            nc.vector.tensor_copy(Wg_hi[:], Wg_par).then_inc(Wg_hi_set, 1)
            dve.wait_ge(Wg_hi_set, 1)
            nc.vector.tensor_tensor(Wg_lo[:], Wg_par, Wg_hi[:], ALU.subtract).then_inc(Wg_lo_set, 1)

            for c in range(NC):
                dve.wait_ge(xnT_ready, c + 1)
                nc.vector.bn_stats(stats_s[:, c, :], xnT_ps[c][:, 0:T]).then_inc(stats_s_set, 1)
                dve.wait_ge(stats_s_set, c + 1)
                nc.vector.bn_aggr(mv_s[:, c, :], stats_s[:, c, :]).then_inc(mv_s_set, 1)
            dve.wait_ge(row_sums_set, 1)
            dve.wait_ge(G_ready, 1)
            G = proj_ps[:, 0:NC * R].rearrange("p (c t r) -> p c t r", c=NC, t=NT)
            for c in range(NC):
                dve.wait_ge(mv_s_set, c + 1)
                nc.vector.scalar_tensor_tensor(
                    out=neg_g[:, c, :].rearrange("p (t r) -> p t r", t=NT), in0=row_sums[:, :, 0, :],
                    scalar=mv_s[:, c, 0:1], in1=G[:, c, :, :],
                    op0=ALU.mult, op1=ALU.subtract).then_inc(neg_g_set, 1)
            for c in range(NC):
                dve.wait_ge(neg_g_set, c + 1)
                dve.wait_ge(rstd_s_set, c + 1)
                nc.vector.scalar_tensor_tensor(
                    out=neg_z[:, c, :].rearrange("p (t r) -> p t r", t=NT),
                    in0=neg_g[:, c, :].rearrange("p (t r) -> p t r", t=NT),
                    scalar=rstd_s[:, c:c + 1], in1=row_sums[:, :, 1, :],
                    op0=ALU.mult, op1=ALU.subtract).then_inc(neg_z_set, 1)
            nc.vector.scalar_tensor_tensor(out=shift_s[:], in0=mv_s[:, NC - 1, 0:1], scalar=-1.0,
                                           in1=rstd_s[:, NC - 1:NC], op0=ALU.mult,
                                           op1=ALU.mult).then_inc(shift_s_set, 1)
            dve.wait_ge(neg_z_set, NC)
            nc.vector.scalar_tensor_tensor(out=neg_abs_z[:], in0=neg_z[:], scalar=-1.0, in1=neg_z[:],
                                           op0=ALU.mult, op1=ALU.min).then_inc(neg_abs_z_set, 1)
            for c in range(NC - 1):
                nc.vector.tensor_scalar(q[:, c, :], xnT_ps[c][:, 0:T], mv_s[:, c, 0:1], rstd_s[:, c:c + 1],
                                        ALU.subtract, ALU.mult).then_inc(q_set[c], 1)
            dve.wait_ge(log1p_set, 1)
            nc.vector.scalar_tensor_tensor(out=neg_dt[:], in0=neg_z[:], scalar=0.0, in1=log1p[:],
                                           op0=ALU.min, op1=ALU.subtract).then_inc(neg_dt_set, 1)
            dve.wait_ge(neg_dt_set, 1)
            dve.wait_ge(A_set, 1)
            nc.vector.tensor_tensor(log_a[:], neg_dt[:], A_row[:].unsqueeze(1).broadcast_to([P, NC, R]),
                                    ALU.mult).then_inc(log_a_set, 1)
            for t in range(NT):
                dve.wait_ge(qT_ready, t + 1)
                nc.vector.tensor_scalar(x_norm[:, t, :], qT_ps[t][:, 0:C], ln_col[:, 2 * t:2 * t + 1],
                                        ln_col[:, 2 * t + 1:2 * t + 2], ALU.mult, ALU.add
                                        ).then_inc(x_norm_set, 1)

            def scan(t):
                dve.wait_ge(decay_ready, t + 1)
                dve.wait_ge(x_norm_set, t + 1)
                nc.vector.tensor_tensor_scan(y[:, t, :], decay_ps[t][:, 0:C], x_norm[:, t, :], 0.0,
                                             ALU.mult, ALU.add).then_inc(y_set, 1)

            def residual(t):
                dve.wait_ge(y_set, t + 1)
                nc.vector.tensor_tensor(x1[:, t, :], y[:, t, :], x_tok[:, t, :], ALU.add).then_inc(x1_set, 1)

            def token_stats(t):
                dve.wait_ge(x1_set, t + 1)
                nc.vector.bn_stats(stats_t[:, t, :], x1[:, t, :]).then_inc(stats_t_set, 1)

            def token_center(t):
                dve.wait_ge(stats_t_set, t + 1)
                nc.vector.bn_aggr(mv_t[:, t, :], stats_t[:, t, :]).then_inc(mv_t_set, 1)
                dve.wait_ge(mv_t_set, t + 1)
                nc.vector.tensor_scalar(xc[:, t, :], x1[:, t, :], mv_t[:, t, 0:1], None,
                                        ALU.subtract).then_inc(xc_set, 1)

            def low_xcT(t):
                dve.wait_ge(xcT_hi_set, t + 1)
                nc.vector.tensor_tensor(xcT_lo[:, t, :, :].rearrange("p c t -> p (c t)"),
                                        xcT_ps[t][:, 0:C],
                                        xcT_hi[:, t, :, :].rearrange("p c t -> p (c t)"),
                                        ALU.subtract).then_inc(xcT_lo_set, 1)

            def top_logits(t):
                dve.wait_ge(logits_ready, t + 1)
                nc.vector.max(top[:, t, :], gate_ps[t][:, 0:E]).then_inc(top_set, 1)
                dve.wait_ge(top_set, t + 1)
                nc.vector.tensor_tensor(gap[:, t:t + 1], top[:, t, 1:2], top[:, t, 0:1],
                                        ALU.subtract).then_inc(gap_set, 1)
                nc.vector.max_index(top_id[:, t, :], top[:, t, :], gate_ps[t][:, 0:E]).then_inc(top_id_set, 1)

            def top_ids(t):
                dve.wait_ge(top_id_set, t + 1)
                nc.vector.tensor_copy(top_idf[:, t, :], top_id[:, t, 0:2]).then_inc(top_idf_set, 1)

            def pick_first(t):
                dve.wait_ge(top_idf_set, t + 1)
                nc.vector.tensor_scalar(first[:, t, :], expert_id, top_idf[:, t, 0:1], None,
                                        ALU.is_equal).then_inc(first_set, 1)

            def pick_second(t):
                dve.wait_ge(e2_set, t + 1)
                nc.vector.tensor_scalar(den[:, t:t + 1], e2[:, t:t + 1], 1.0, None,
                                        ALU.add).then_inc(den_set, 1)
                nc.vector.tensor_scalar(second[:, t, :], expert_id, top_idf[:, t, 1:2], e2[:, t:t + 1],
                                        ALU.is_equal, ALU.mult).then_inc(second_set, 1)

            def join_picks(t):
                dve.wait_ge(den_set, t + 1)
                nc.vector.reciprocal(g1[:, t:t + 1], den[:, t:t + 1]).then_inc(g1_set, 1)
                dve.wait_ge(first_set, t + 1)
                dve.wait_ge(second_set, t + 1)
                nc.vector.tensor_tensor(picks[:, t, :], first[:, t, :], second[:, t, :],
                                        ALU.add).then_inc(picks_set, 1)

            def gates(t):
                dve.wait_ge(picks_set, t + 1)
                dve.wait_ge(g1_set, t + 1)
                dve.wait_ge(rstd_t_set, t + 1)
                nc.vector.tensor_scalar(gate_rstd[:, t, :], picks[:, t, :], g1[:, t:t + 1],
                                        rstd_t[:, t:t + 1], ALU.mult, ALU.mult).then_inc(gate_rstd_set, 1)
                nc.vector.tensor_scalar(gate[:, t, :], picks[:, t, :], g1[:, t:t + 1], None,
                                        ALU.mult).then_inc(gate_set, 1)

            def add_expert(t, e):
                total = sum_odd if e in (1, 3) else sum_even
                dve.wait_ge(gate_rstd_set, t + 1)
                dve.wait_ge(y_ready[t], e + 1)
                if e == 1:
                    nc.vector.tensor_scalar(total[:, t, :], y_ps[t][e], gate_rstd[:, t, e:e + 1], None,
                                            ALU.mult).then_inc(summed[t], 1)
                    return
                if e > 1:
                    dve.wait_ge(summed[t], step[{2: 0, 3: 1, 4: "join"}.get(e, e - 1)])
                nc.vector.scalar_tensor_tensor(
                    out=total[:, t, :], in0=y_ps[t][e], scalar=gate_rstd[:, t, e:e + 1],
                    in1=(total if e else x1)[:, t, :],
                    op0=ALU.mult, op1=ALU.add).then_inc(summed[t], 1)

            def add_bias(t):
                dve.wait_ge(bias_ready, t + 1)
                dve.wait_ge(summed[t], step[2])
                nc.vector.tensor_tensor(sum_even[:, t, :], sum_even[:, t, :], gate_ps[t][:, 0:H],
                                        ALU.add).then_inc(summed[t], 1)

            def join_sums(t):
                dve.wait_ge(summed[t], step["bias"])
                nc.vector.tensor_tensor(sum_even[:, t, :], sum_even[:, t, :], sum_odd[:, t, :],
                                        ALU.add).then_inc(summed[t], 1)

            scan(0)
            residual(0)
            token_stats(0)
            token_center(0)
            scan(1)
            residual(1)
            token_stats(1)
            low_xcT(0)
            token_center(1)
            low_xcT(1)
            top_logits(0)
            top_ids(0)
            pick_first(0)
            pick_second(0)
            join_picks(0)
            gates(0)
            add_expert(0, 0)
            add_expert(0, 1)
            top_logits(1)
            add_expert(0, 2)
            top_ids(1)
            add_expert(0, 3)
            pick_first(1)
            pick_second(1)
            add_bias(0)
            join_picks(1)
            join_sums(0)
            gates(1)
            for e in range(4, E):
                add_expert(0, e)
            for e in range(4):
                add_expert(1, e)
            add_bias(1)
            join_sums(1)
            for e in range(4, E):
                add_expert(1, e)


def kernel(**inputs):
    import numpy as np
    import concourse.bacc as bacc
    from concourse.bass_utils import run_bass_kernel_spmd

    def given(name):
        return np.ascontiguousarray(inputs[name])

    x = given("x")
    _, C, R, _ = x.shape
    T = R * R
    NT, ROWS = T // P, P // R
    We, Wg = given("L0_ffn_We"), given("L0_ffn_Wg")
    E, D, H = We.shape
    at, n_params = param_columns(C, R, E)
    params = np.zeros((P, n_params), np.float32)
    params[:, at["ident"]] = np.eye(P, dtype=np.float32)
    params[:, at["row_mask"]] = np.repeat(np.eye(ROWS, dtype=np.float32), R, axis=0)
    params[:, at["expert_id"]] = np.arange(E, dtype=np.float32)
    for t in range(NT):
        for k, name in enumerate(("L0_conv_ln_w", "L0_conv_ln_b")):
            params[:, at["ln"].start + 2 * t + k] = given(name).reshape(NT, P)[t]
    params[:, at["dt_w"]] = np.tile(given("L0_conv_dt_w").reshape(R, 1), (ROWS, 1))
    params[:, at["dt_b"]].reshape(P, NT, 2, ROWS)[:, :, 1, :] = given("L0_conv_dt_b")[0]
    params[:, at["log_A"]] = given("L0_conv_log_A")
    params[:, at["Wg"]] = Wg.reshape(C // P, P, E).transpose(1, 0, 2).reshape(P, -1)
    arrays = {
        "x_tokens": np.ascontiguousarray(x.reshape(C, T).T),
        "params": params,
        "We_rows": np.ascontiguousarray(We.transpose(1, 0, 2)).reshape(D, E * H),
        "be": given("L0_ffn_be"),
    }

    nc = bacc.Bacc("TRN2", target_bir_lowering=False, num_devices=1)
    dram = {name: nc.dram_tensor(f"in_{name}", a.shape, F32, kind="ExternalInput").ap()
            for name, a in arrays.items()}
    out = nc.dram_tensor("out_tokens", (T, C), F32, kind="ExternalOutput").ap()
    metaformer_block(nc, dram["x_tokens"], dram["params"], dram["We_rows"], dram["be"], out)
    result = run_bass_kernel_spmd(nc, [{f"in_{name}": a for name, a in arrays.items()}], core_ids=[0])
    return np.ascontiguousarray(result.results[0]["out_tokens"].T).reshape(1, C, R, R)
```

```python
from contextlib import ExitStack

import concourse.bass as bass
from concourse import mybir

F32 = mybir.dt.float32
F32R = mybir.dt.float32r
BF16 = mybir.dt.bfloat16
U32 = mybir.dt.uint32
ALU = mybir.AluOpType
ACT = mybir.ActivationFunctionType

P = 128
EPS_CHANNEL = 1e-6
EPS_SPATIAL = 1e-5
EPS_TOKEN = 1e-5
WARM_START, WARM_Z, WARM_SCAN = 10, 6, 6
POOL_PAIRS = (0, 1, 3)


def param_columns(C, R, E):
    NT, NC, ROWS = R * R // P, C // P, P // R
    at, start = {}, 0
    for name, width in (("ident", P), ("row_mask", ROWS), ("expert_id", E), ("ln", NT * 2), ("dt_w", 1),
                        ("dt_b", NT * 2 * ROWS), ("log_A", R), ("Wg", NC * E)):
        at[name] = slice(start, start + width)
        start += width
    return at, start


def metaformer_block(nc, x, params, We, be, out):
    T, C = x.shape
    E, D, H = be.shape[0], We.shape[0], be.shape[1]
    R = int(T ** 0.5)
    NT = T // P
    NC = C // P
    ROWS = P // R
    PAIR = 2
    NPAIR = E // PAIR
    assert R * R == T == NT * P and C == NC * P == D == H and PAIR * H == 512 and E == 8
    assert NC == 2 and NT == 2

    at, n_params = param_columns(C, R, E)
    x_dram = x.rearrange("(t p) c -> p t c", p=P)
    out_dram = out.rearrange("(t p) c -> p t c", p=P)
    We_dram = We.rearrange("(c p) (e h) -> p c e h", p=P, e=E)

    with ExitStack() as ctx:
        def sb(name, shape, dt=F32):
            return ctx.enter_context(nc.sbuf_tensor(name, shape, dt))

        def sem(name):
            return ctx.enter_context(nc.semaphore(name))

        x_tok = sb("x_tok", [P, NT, C])
        par = sb("par", [P, n_params])
        be_sb = sb("be_sb", [E, H])
        We_sb = sb("We_sb", [P, NC, E, H])
        ident = par[:, at["ident"]]
        row_mask = par[:, at["row_mask"]]
        expert_id = par[:, at["expert_id"]]
        ln_col = par[:, at["ln"]]
        dtw_col = par[:, at["dt_w"]]
        dtb_row = par[:, at["dt_b"]]
        logA_row = par[:, at["log_A"]]
        Wg_par = par[:, at["Wg"]].rearrange("p (c e) -> p c e", c=NC)
        ones = sb("ones", [P, P])
        one_bf16 = nc.const_aps.tensor(1.0, [P, 1], BF16)
        eps_channel = sb("eps_channel", [P, 1])
        eps_spatial = sb("eps_spatial", [P, 1])
        eps_token = sb("eps_token", [P, 1])
        one_col = sb("one_col", [P, 1])
        A_row = sb("A_row", [P, R])
        proj = sb("proj", [P, NT, 2, ROWS])
        row_sums = sb("row_sums", [P, NT, 2, ROWS])
        W_hi = sb("W_hi", [P, NC, E * H + E], F32R)
        W_lo = sb("W_lo", [P, NC, E * H + E], F32R)
        Wg_hi, Wg_lo = W_hi[:, :, H:H + E], W_lo[:, :, H:H + E]
        stats_c = sb("stats_c", [P, NT, 6])
        mv_c = sb("mv_c", [P, NT, 2])
        lnv_c = sb("lnv_c", [P, NT])
        rstd_c = sb("rstd_c", [P, NT])
        xn = sb("xn", [P, NT, C])
        stats_s = sb("stats_s", [P, NC, NT, 6])
        mv_s = sb("mv_s", [P, NC, 2])
        lnv_s = sb("lnv_s", [P, NC])
        rstd_s = sb("rstd_s", [P, NC])
        shift_s = sb("shift_s", [P, 1])
        q = sb("q", [P, NC, T])
        x_norm = sb("x_norm", [P, NT, C])
        neg_g = sb("neg_g", [P, NC, R])
        neg_z = sb("neg_z", [P, NC, R])
        neg_abs_z = sb("neg_abs_z", [P, NC, R])
        exp_abs = sb("exp_abs", [P, NC, R])
        log1p = sb("log1p", [P, NC, R])
        neg_dt = sb("neg_dt", [P, NC, R])
        log_a = sb("log_a", [P, NC, R])
        decay = sb("decay", [P, NT, NC, P])
        y = sb("y", [P, NT, C])
        x1 = sb("x1", [P, NT, C])
        x1_sum = sb("x1_sum", [P, NT])
        xc_square = sb("xc_square", [P, C])
        square_sum = sb("square_sum", [P, NT])
        lnv_t = sb("lnv_t", [P, NT])
        rstd_t = sb("rstd_t", [P, NT])
        xc = sb("xc", [P, NT, C])
        xcT_hi = sb("xcT_hi", [P, NT, NC, P], F32R)
        xcT_lo = sb("xcT_lo", [P, NT, NC, P], F32R)
        top = sb("top", [P, NT, E])
        top_id = sb("top_id", [P, NT, E], U32)
        top_idf = sb("top_idf", [P, NT, 2])
        gap = sb("gap", [P, NT])
        e2 = sb("e2", [P, NT])
        den = sb("den", [P, NT])
        g1 = sb("g1", [P, NT])
        first = sb("first", [P, NT, E])
        second = sb("second", [P, NT, E])
        picks = sb("picks", [P, NT, E])
        gate = sb("gate", [P, NT, E])
        gate_rstd = sb("gate_rstd", [P, NT, E])
        gateT = sb("gateT", [E, NT, P])
        total = sb("total", [P, NT, H])
        aside = sb("aside", [P, NT, 3, H])

        all_banks = ctx.enter_context(nc.psum_tensor("banks", [P, 8, 512], F32))
        banks = [all_banks[:, i, :] for i in range(8)]
        xnT_ps = [all_banks[:, c * NT:(c + 1) * NT, 0:P] for c in range(NC)]
        decay_ps = banks[0:2]
        qT_ps = banks[6:8]
        xcT_ps = banks[2:4]
        sums_ps = banks[6]
        proj_ps = banks[4]
        gate_ps = banks[4:6]
        warm_ps = banks[5]
        y_at = [[(6, 0), (7, 0), (0, 0), (0, H), (2, 0), (2, H), (3, 0), (3, H)],
                [(1, 0), (6, 0), (7, 0), (4, 0), (0, 0), (2, 0), (6, 0), (3, 0)]]
        y_ps = [[banks[b][:, h:h + H] for b, h in y_at[t]] for t in range(NT)]
        logits_ps = [banks[y_at[t][0][0]][:, H:H + E] for t in range(NT)]

        x_in = [sem(f"x_in{t}") for t in range(NT)]
        par_in = sem("par_in")
        be_in = sem("be_in")
        We_in = [sem(f"We_in{p}") for p in range(NPAIR)]
        out_done = sem("out_done")

        const_set = sem("const_set")
        A_set = sem("A_set")
        proj_set = sem("proj_set")
        sums_ready = sem("sums_ready")
        row_sums_set = sem("row_sums_set")
        W_hi_set = sem("W_hi_set")
        W_lo_set = [sem(f"W_lo_set{p}") for p in range(NPAIR)]
        Wg_hi_set = sem("Wg_hi_set")
        Wg_lo_set = sem("Wg_lo_set")

        stats_c_set = sem("stats_c_set")
        mv_c_set = sem("mv_c_set")
        lnv_c_set = sem("lnv_c_set")
        rstd_c_set = sem("rstd_c_set")
        xn_set = sem("xn_set")
        xnT_ready = sem("xnT_ready")
        G_ready = sem("G_ready")
        stats_s_set = sem("stats_s_set")
        mv_s_set = sem("mv_s_set")
        lnv_s_set = sem("lnv_s_set")
        rstd_s_set = sem("rstd_s_set")
        shift_s_set = sem("shift_s_set")
        q_set = [sem(f"q_set{c}") for c in range(NC)]
        qT_ready = sem("qT_ready")
        x_norm_set = [sem(f"x_norm_set{t}") for t in range(NT)]
        neg_g_set = sem("neg_g_set")
        neg_z_set = sem("neg_z_set")
        neg_abs_z_set = sem("neg_abs_z_set")
        exp_abs_set = sem("exp_abs_set")
        log1p_set = sem("log1p_set")
        neg_dt_set = sem("neg_dt_set")
        log_a_set = sem("log_a_set")
        decay_set = sem("decay_set")
        decay_ready = sem("decay_ready")
        y_set = sem("y_set")
        x1_set = sem("x1_set")
        square_sum_set = sem("square_sum_set")
        lnv_t_set = sem("lnv_t_set")
        rstd_t_set = sem("rstd_t_set")
        xc_set = sem("xc_set")
        xcT_ready = sem("xcT_ready")
        xcT_hi_set = sem("xcT_hi_set")
        xcT_lo_set = sem("xcT_lo_set")
        top_set = sem("top_set")
        top_id_set = sem("top_id_set")
        top_idf_set = sem("top_idf_set")
        gap_set = sem("gap_set")
        e2_set = sem("e2_set")
        den_set = sem("den_set")
        g1_set = sem("g1_set")
        first_set = sem("first_set")
        second_set = sem("second_set")
        picks_set = sem("picks_set")
        gate_set = sem("gate_set")
        gate_rstd_set = sem("gate_rstd_set")
        gateT_ready = sem("gateT_ready")
        gateT_set = sem("gateT_set")
        bias_ready = sem("bias_ready")
        aside_set = [sem(f"aside_set{t}") for t in range(NT)]
        aside_sum = [sem(f"aside_sum{t}") for t in range(NT)]
        y_ready = [sem(f"y_ready{t}") for t in range(NT)]
        summed = [sem(f"summed{t}") for t in range(NT)]
        ASIDE = [(1, 3), (1, 2)]
        assert all(len(a) == 2 for a in ASIDE)
        order = [[0, 2, 4, 5, 6, 7, "join"], [0, 3, 4, "join", 5, 6, 7]]
        step = [{what: n + 1 for n, what in enumerate(o)} for o in order]
        STEPS = len(order[0])

        def columns(e0, e1):
            return slice(e0 * H + E if e0 else 0, e1 * H + E)

        def pair_columns(w, p, c):
            if p:
                return w[:, c, columns(p * PAIR, (p + 1) * PAIR)].rearrange("p (e h) -> p e h", e=PAIR)
            return w[:, c, 0:PAIR * (H + E)].rearrange("p (e h) -> p e h", e=PAIR)[:, :, 0:H]

        block = ctx.enter_context(nc.Block())

        @block.sync
        def _(sp):
            for t in range(NT):
                sp.dma_start(x_tok[:, t, :], x_dram[:, t, :]).then_inc(x_in[t], 16)
            sp.dma_start(par[:], params).then_inc(par_in, 16)
            for p in range(NPAIR):
                pair = slice(p * PAIR, (p + 1) * PAIR)
                sp.dma_start(We_sb[:, :, pair, :].rearrange("p c e h -> p c (e h)"),
                             We_dram[:, :, pair, :].rearrange("p c e h -> p c (e h)")).then_inc(We_in[p], 16)
            sp.dma_start(be_sb[:], be).then_inc(be_in, 16)
            for t in range(NT):
                sp.wait_ge(summed[t], STEPS)
                sp.dma_start(out_dram[:, t, :], total[:, t, :]).then_inc(out_done, 16)
            sp.wait_ge(out_done, 16 * NT)

        @block.gpsimd
        def _(pool):
            for p in POOL_PAIRS:
                if p:
                    pool.wait_ge(log_a_set, 1)
                for c in range(NC):
                    pool.wait_ge(W_hi_set, p * NC + c + 1)
                    for e in range(PAIR):
                        nc.gpsimd.tensor_tensor(pair_columns(W_lo, p, c)[:, e, :],
                                                We_sb[:, c, p * PAIR + e, :],
                                                pair_columns(W_hi, p, c)[:, e, :],
                                                ALU.subtract).then_inc(W_lo_set[p], 1)
            for t in range(NT):
                pool.wait_ge(aside_set[t], 2)
                nc.gpsimd.tensor_tensor(aside[:, t, 0, :], aside[:, t, 0, :], aside[:, t, 1, :],
                                        ALU.add).then_inc(aside_sum[t], 1)
                pool.wait_ge(aside_set[t], 3)
                pool.wait_ge(aside_sum[t], 1)
                nc.gpsimd.tensor_tensor(aside[:, t, 0, :], aside[:, t, 0, :], aside[:, t, 2, :],
                                        ALU.add).then_inc(aside_sum[t], 1)

        @block.tensor
        def _(pe):
            def transpose(dst, src):
                return pe.transpose(dst, src, ident)

            def keep_warm(n):
                for _ in range(n):
                    pe.matmul(warm_ps, one_bf16.broadcast_to([P, P]), one_bf16.broadcast_to([P, 512]),
                              start=True, stop=True)

            keep_warm(WARM_START)

            def xn_transposes(t):
                pe.wait_ge(xn_set, t + 1)
                for c in range(NC):
                    mm = transpose(xnT_ps[c][:, t, :], xn[:, t, c * P:(c + 1) * P])
                mm.then_inc(xnT_ready, 1)

            def project(c, t):
                at = (c * NT + t) * ROWS
                return pe.matmul(proj_ps[:, at:at + ROWS], xn[:, t, c * P:(c + 1) * P],
                                 proj[:, t, 0, :], start=True, stop=True)

            pe.wait_ge(const_set, 1)
            pe.wait_ge(proj_set, 1)
            for t in range(NT):
                mm = pe.matmul(sums_ps[:, t * 2 * ROWS:(t + 1) * 2 * ROWS], ones[:],
                               proj[:, t, :, :].rearrange("p k r -> p (k r)"), start=True, stop=True)
            mm.then_inc(sums_ready, 1)
            xn_transposes(0)
            project(0, 0)
            xn_transposes(1)
            project(1, 0)
            project(0, 1)
            project(1, 1).then_inc(G_ready, 1)
            keep_warm(WARM_Z)
            for c in range(NC):
                pe.wait_ge(q_set[c], 1)
                for t in range(NT):
                    mm = transpose(qT_ps[c][:, t * P:(t + 1) * P], q[:, c, t * P:(t + 1) * P])
                mm.then_inc(qT_ready, 1)
            for t in range(NT):
                pe.wait_ge(decay_set, t + 1)
                for c in range(NC):
                    mm = transpose(decay_ps[t][:, c * P:(c + 1) * P], decay[:, t, c, :])
                mm.then_inc(decay_ready, 1)
            keep_warm(WARM_SCAN)

            def center_transposes(t):
                pe.wait_ge(xc_set, t + 1)
                if t:
                    pe.wait_ge(xcT_lo_set, t)
                else:
                    for n in range(NT):
                        pe.wait_ge(x_norm_set[n], NC)
                for c in range(NC):
                    transpose(xcT_ps[c][:, t * P:(t + 1) * P],
                              xc[:, t, c * P:(c + 1) * P]).then_inc(xcT_ready, 1)

            def expert(t, *experts):
                p = experts[0] // PAIR
                cols = columns(experts[0], experts[-1] + 1)
                bank, start = y_at[t][experts[0]]
                dst = banks[bank][:, start:start + cols.stop - cols.start]
                if experts[0] == 0:
                    pe.wait_ge(Wg_hi_set, 1)
                    pe.wait_ge(Wg_lo_set, 1)
                products = [(xcT_hi, W_hi), (xcT_hi, W_lo), (xcT_lo, W_hi)]
                for k, (left, right) in enumerate(products):
                    if right is W_hi:
                        pe.wait_ge(W_hi_set, (p + 1) * NC)
                    else:
                        pe.wait_ge(W_lo_set[p], NC * PAIR if p in POOL_PAIRS else NC)
                    if left is xcT_lo:
                        pe.wait_ge(xcT_lo_set, t + 1)
                    for c in range(NC):
                        if left is xcT_hi:
                            pe.wait_ge(xcT_hi_set, t * NC + c + 1)
                        mm = pe.matmul(dst, left[:, t, c, :], right[:, c, cols],
                                       start=(k == 0 and c == 0),
                                       stop=(k == len(products) - 1 and c == NC - 1))
                mm.then_inc(y_ready[t], len(experts))

            def gate_transpose(t):
                pe.wait_ge(gate_set, t + 1)
                transpose(gate_ps[t][0:E, 0:P], gate[:, t, :]).then_inc(gateT_ready, 1)

            def gate_bias(t):
                pe.wait_ge(be_in, 16)
                pe.wait_ge(gateT_set, t + 1)
                pe.matmul(gate_ps[t][:, 0:H], gateT[:, t, :], be_sb[:], start=True,
                          stop=True).then_inc(bias_ready, 1)

            center_transposes(0)
            keep_warm(1)
            expert(0, 0)
            expert(0, 1)
            center_transposes(1)
            pe.wait_ge(y_set, NT)
            expert(0, 2, 3)
            expert(1, 0)
            pe.wait_ge(xcT_lo_set, NT)
            expert(0, 4, 5)
            gate_transpose(0)
            expert(0, 6, 7)
            pe.wait_ge(summed[0], step[0][0])
            expert(1, 1)
            gate_transpose(1)
            gate_bias(0)
            pe.wait_ge(aside_set[0], 1)
            expert(1, 2)
            gate_bias(1)
            pe.wait_ge(aside_set[0], 3)
            expert(1, 3)
            expert(1, 4)
            pe.wait_ge(summed[0], step[0][5])
            expert(1, 5)
            pe.wait_ge(aside_set[1], 1)
            expert(1, 6)
            pe.wait_ge(summed[0], step[0][7])
            expert(1, 7)

        @block.scalar
        def _(act):
            nc.scalar.preload_act_table_set("natural_log_exp_and_others")
            act.wait_ge(const_set, 1)

            def rsqrt(rstd, lnv, var, eps, lnv_set, n, rstd_set, scale=1.0):
                nc.scalar.activation(lnv, var, ACT.Ln, bias=eps[:], scale=scale).then_inc(lnv_set, 1)
                act.wait_ge(lnv_set, n)
                nc.scalar.activation(rstd, lnv, ACT.Exp, scale=-0.5).then_inc(rstd_set, 1)

            def round_W(p, c):
                act.wait_ge(We_in[p], 16)
                nc.scalar.copy(pair_columns(W_hi, p, c),
                               We_sb[:, c, p * PAIR:(p + 1) * PAIR, :]).then_inc(W_hi_set, 1)

            for t in range(NT):
                act.wait_ge(mv_c_set, t + 1)
                rsqrt(rstd_c[:, t:t + 1], lnv_c[:, t:t + 1], mv_c[:, t, 1:2], eps_channel,
                      lnv_c_set, t + 1, rstd_c_set)
            act.wait_ge(par_in, 16)
            nc.scalar.activation(A_row[:], logA_row, ACT.Exp).then_inc(A_set, 1)
            round_W(0, 0)
            round_W(0, 1)
            for c in range(NC):
                act.wait_ge(mv_s_set, c + 1)
                nc.scalar.activation(lnv_s[:, c:c + 1], mv_s[:, c, 1:2], ACT.Ln,
                                     bias=eps_spatial[:]).then_inc(lnv_s_set, 1)
            for c in range(NC):
                act.wait_ge(lnv_s_set, c + 1)
                nc.scalar.activation(rstd_s[:, c:c + 1], lnv_s[:, c:c + 1], ACT.Exp,
                                     scale=-0.5).then_inc(rstd_s_set, 1)
            round_W(1, 0)
            act.wait_ge(neg_abs_z_set, 1)
            nc.scalar.activation(exp_abs[:], neg_abs_z[:], ACT.Exp).then_inc(exp_abs_set, 1)
            act.wait_ge(exp_abs_set, 1)
            nc.scalar.activation(log1p[:], exp_abs[:], ACT.Ln, bias=one_col[:]).then_inc(log1p_set, 1)
            act.wait_ge(shift_s_set, 1)
            nc.scalar.activation(q[:, NC - 1, :].rearrange("p (t k) -> p t k", t=NT),
                                 xnT_ps[NC - 1], ACT.Identity,
                                 bias=shift_s[:], scale=rstd_s[:, NC - 1:NC]).then_inc(q_set[NC - 1], 1)
            act.wait_ge(log_a_set, 1)
            for t in range(NT):
                rows = log_a[:, :, t * ROWS:(t + 1) * ROWS]
                nc.scalar.activation(decay[:, t, :, :].rearrange("p c (r k) -> p c r k", k=R),
                                     rows.unsqueeze(3).broadcast_to([P, NC, ROWS, R]),
                                     ACT.Exp).then_inc(decay_set, 1)
            t = NT - 1
            for c in range(NC):
                act.wait_ge(qT_ready, c + 1)
                act.wait_ge(x_norm_set[0], c + 1)
                nc.scalar.activation(x_norm[:, t, c * P:(c + 1) * P], qT_ps[c][:, t * P:(t + 1) * P],
                                     ACT.Identity, bias=ln_col[:, 2 * t + 1:2 * t + 2],
                                     scale=ln_col[:, 2 * t:2 * t + 1]).then_inc(x_norm_set[t], 1)
            round_W(1, 1)
            round_W(2, 0)

            def token_rsqrt(t):
                act.wait_ge(xc_set, t + 1)
                nc.scalar.activation(xc_square[:], xc[:, t, :], ACT.Square,
                                     accum_out=square_sum[:, t:t + 1]).then_inc(square_sum_set, 1)
                act.wait_ge(square_sum_set, t + 1)
                rsqrt(rstd_t[:, t:t + 1], lnv_t[:, t:t + 1], square_sum[:, t:t + 1], eps_token,
                      lnv_t_set, t + 1, rstd_t_set, scale=1.0 / C)

            def round_xcT(t):
                for c in range(NC):
                    act.wait_ge(xcT_ready, t * NC + c + 1)
                    nc.scalar.copy(xcT_hi[:, t, c, :],
                                   xcT_ps[c][:, t * P:(t + 1) * P]).then_inc(xcT_hi_set, 1)

            def second_exp(t):
                act.wait_ge(gap_set, t + 1)
                act.wait_ge(rstd_t_set, t + 1)
                nc.scalar.activation(e2[:, t:t + 1], gap[:, t:t + 1], ACT.Exp,
                                     scale=rstd_t[:, t:t + 1]).then_inc(e2_set, 1)

            def copy_gateT(t):
                act.wait_ge(gateT_ready, t + 1)
                nc.scalar.copy(gateT[:, t, :], gate_ps[t][0:E, 0:P]).then_inc(gateT_set, 1)

            def scale_aside(t, n):
                e = ASIDE[t][n]
                act.wait_ge(gate_rstd_set, t + 1)
                act.wait_ge(y_ready[t], e + 1)
                if y_at[t][e][0] == y_at[t][e - 1][0]:
                    act.wait_ge(summed[t], step[t][e - 1])
                nc.scalar.activation(aside[:, t, n, :], y_ps[t][e], ACT.Identity,
                                     scale=gate_rstd[:, t, e:e + 1]).then_inc(aside_set[t], 1)

            def copy_bias(t):
                act.wait_ge(bias_ready, t + 1)
                nc.scalar.copy(aside[:, t, len(ASIDE[t]), :], gate_ps[t][:, 0:H]).then_inc(aside_set[t], 1)

            round_xcT(0)
            token_rsqrt(0)
            round_W(2, 1)
            round_W(3, 0)
            second_exp(0)
            round_xcT(1)
            round_W(3, 1)
            token_rsqrt(1)

            scale_aside(0, 0)
            second_exp(1)
            scale_aside(0, 1)
            copy_gateT(0)
            scale_aside(1, 0)
            copy_gateT(1)
            copy_bias(0)
            scale_aside(1, 1)
            copy_bias(1)

        @block.vector
        def _(dve):
            nc.vector.memset(ones[:], 1.0)
            nc.vector.memset(eps_channel[:], EPS_CHANNEL)
            nc.vector.memset(eps_spatial[:], EPS_SPATIAL)
            nc.vector.memset(eps_token[:], EPS_TOKEN)
            nc.vector.memset(one_col[:], 1.0).then_inc(const_set, 1)

            def channel_stats(t):
                dve.wait_ge(x_in[t], 16)
                nc.vector.bn_stats(stats_c[:, t, :], x_tok[:, t, :]).then_inc(stats_c_set, 1)
                dve.wait_ge(stats_c_set, t + 1)
                nc.vector.bn_aggr(mv_c[:, t, :], stats_c[:, t, :]).then_inc(mv_c_set, 1)

            def channel_norm(t):
                dve.wait_ge(mv_c_set, t + 1)
                dve.wait_ge(rstd_c_set, t + 1)
                nc.vector.tensor_scalar(xn[:, t, :], x_tok[:, t, :], mv_c[:, t, 0:1], rstd_c[:, t:t + 1],
                                        ALU.subtract, ALU.mult).then_inc(xn_set, 1)

            channel_stats(0)
            channel_stats(1)
            dve.wait_ge(par_in, 16)
            nc.vector.scalar_tensor_tensor(
                out=proj[:].rearrange("p t k r -> p (t k) r"),
                in0=ln_col.unsqueeze(2).broadcast_to([P, NT * 2, ROWS]), scalar=dtw_col,
                in1=row_mask.unsqueeze(1).broadcast_to([P, NT * 2, ROWS]),
                op0=ALU.mult, op1=ALU.mult).then_inc(proj_set, 1)
            nc.vector.tensor_copy(Wg_hi, Wg_par).then_inc(Wg_hi_set, 1)
            channel_norm(0)
            dve.wait_ge(Wg_hi_set, 1)
            nc.vector.tensor_tensor(Wg_lo, Wg_par, Wg_hi, ALU.subtract).then_inc(Wg_lo_set, 1)
            channel_norm(1)
            dve.wait_ge(sums_ready, 1)
            nc.vector.tensor_tensor(row_sums[:].rearrange("p t k r -> p (t k r)"), dtb_row,
                                    sums_ps[:, 0:NT * 2 * ROWS], ALU.add).then_inc(row_sums_set, 1)

            for t in range(NT):
                dve.wait_ge(xnT_ready, t + 1)
                for c in range(NC):
                    nc.vector.bn_stats(stats_s[:, c, t, :], xnT_ps[c][:, t, :]).then_inc(stats_s_set, 1)
            for c in range(NC):
                dve.wait_ge(stats_s_set, (NT - 1) * NC + c + 1)
                nc.vector.bn_aggr(mv_s[:, c, :], stats_s[:, c, :, :].rearrange("p t s -> p (t s)")
                                  ).then_inc(mv_s_set, 1)
            dve.wait_ge(row_sums_set, 1)
            dve.wait_ge(G_ready, 1)
            G = proj_ps[:, 0:NC * R].rearrange("p (c t r) -> p c t r", c=NC, t=NT)
            for c in range(NC):
                dve.wait_ge(mv_s_set, c + 1)
                nc.vector.scalar_tensor_tensor(
                    out=neg_g[:, c, :].rearrange("p (t r) -> p t r", t=NT), in0=row_sums[:, :, 0, :],
                    scalar=mv_s[:, c, 0:1], in1=G[:, c, :, :],
                    op0=ALU.mult, op1=ALU.subtract).then_inc(neg_g_set, 1)
            for c in range(NC):
                dve.wait_ge(neg_g_set, c + 1)
                dve.wait_ge(rstd_s_set, c + 1)
                nc.vector.scalar_tensor_tensor(
                    out=neg_z[:, c, :].rearrange("p (t r) -> p t r", t=NT),
                    in0=neg_g[:, c, :].rearrange("p (t r) -> p t r", t=NT),
                    scalar=rstd_s[:, c:c + 1], in1=row_sums[:, :, 1, :],
                    op0=ALU.mult, op1=ALU.subtract).then_inc(neg_z_set, 1)
            nc.vector.scalar_tensor_tensor(out=shift_s[:], in0=mv_s[:, NC - 1, 0:1], scalar=-1.0,
                                           in1=rstd_s[:, NC - 1:NC], op0=ALU.mult,
                                           op1=ALU.mult).then_inc(shift_s_set, 1)
            dve.wait_ge(neg_z_set, NC)
            nc.vector.scalar_tensor_tensor(out=neg_abs_z[:], in0=neg_z[:], scalar=-1.0, in1=neg_z[:],
                                           op0=ALU.mult, op1=ALU.min).then_inc(neg_abs_z_set, 1)
            for c in range(NC - 1):
                nc.vector.tensor_scalar(q[:, c, :].rearrange("p (t k) -> p t k", t=NT),
                                        xnT_ps[c], mv_s[:, c, 0:1], rstd_s[:, c:c + 1],
                                        ALU.subtract, ALU.mult).then_inc(q_set[c], 1)
            dve.wait_ge(log1p_set, 1)
            nc.vector.scalar_tensor_tensor(out=neg_dt[:], in0=neg_z[:], scalar=0.0, in1=log1p[:],
                                           op0=ALU.min, op1=ALU.subtract).then_inc(neg_dt_set, 1)
            dve.wait_ge(neg_dt_set, 1)
            dve.wait_ge(A_set, 1)
            nc.vector.tensor_tensor(log_a[:], neg_dt[:], A_row[:].unsqueeze(1).broadcast_to([P, NC, R]),
                                    ALU.mult).then_inc(log_a_set, 1)
            for c in range(NC):
                dve.wait_ge(qT_ready, c + 1)
                nc.vector.tensor_scalar(x_norm[:, 0, c * P:(c + 1) * P], qT_ps[c][:, 0:P], ln_col[:, 0:1],
                                        ln_col[:, 1:2], ALU.mult, ALU.add).then_inc(x_norm_set[0], 1)

            def scan(t):
                dve.wait_ge(decay_ready, t + 1)
                dve.wait_ge(x_norm_set[t], NC)
                nc.vector.tensor_tensor_scan(y[:, t, :], decay_ps[t][:, 0:C], x_norm[:, t, :], 0.0,
                                             ALU.mult, ALU.add).then_inc(y_set, 1)

            def residual(t):
                dve.wait_ge(y_set, t + 1)
                nc.vector.tensor_tensor_reduce(x1[:, t, :], y[:, t, :], x_tok[:, t, :], 1.0, 0.0,
                                               ALU.add, ALU.add, x1_sum[:, t:t + 1]).then_inc(x1_set, 1)

            def token_center(t):
                dve.wait_ge(x1_set, t + 1)
                nc.vector.scalar_tensor_tensor(out=xc[:, t, :], in0=x1_sum[:, t:t + 1].broadcast_to([P, C]),
                                               scalar=-1.0 / C, in1=x1[:, t, :], op0=ALU.mult,
                                               op1=ALU.add).then_inc(xc_set, 1)

            def low_W(p, c):
                dve.wait_ge(W_hi_set, p * NC + c + 1)
                nc.vector.tensor_tensor(pair_columns(W_lo, p, c), We_sb[:, c, p * PAIR:(p + 1) * PAIR, :],
                                        pair_columns(W_hi, p, c), ALU.subtract).then_inc(W_lo_set[p], 1)

            def low_xcT(t):
                for c in range(NC):
                    dve.wait_ge(xcT_hi_set, t * NC + c + 1)
                    low = nc.vector.tensor_tensor(xcT_lo[:, t, c, :], xcT_ps[c][:, t * P:(t + 1) * P],
                                                  xcT_hi[:, t, c, :], ALU.subtract)
                low.then_inc(xcT_lo_set, 1)

            def top_logits(t):
                dve.wait_ge(y_ready[t], 1)
                nc.vector.max(top[:, t, :], logits_ps[t]).then_inc(top_set, 1)
                dve.wait_ge(top_set, t + 1)
                nc.vector.tensor_tensor(gap[:, t:t + 1], top[:, t, 1:2], top[:, t, 0:1],
                                        ALU.subtract).then_inc(gap_set, 1)
                nc.vector.max_index(top_id[:, t, :], top[:, t, :], logits_ps[t]).then_inc(top_id_set, 1)

            def top_ids(t):
                dve.wait_ge(top_id_set, t + 1)
                nc.vector.tensor_copy(top_idf[:, t, :], top_id[:, t, 0:2]).then_inc(top_idf_set, 1)

            def pick_first(t):
                dve.wait_ge(top_idf_set, t + 1)
                nc.vector.tensor_scalar(first[:, t, :], expert_id, top_idf[:, t, 0:1], None,
                                        ALU.is_equal).then_inc(first_set, 1)

            def pick_second(t):
                dve.wait_ge(e2_set, t + 1)
                nc.vector.tensor_scalar(den[:, t:t + 1], e2[:, t:t + 1], 1.0, None,
                                        ALU.add).then_inc(den_set, 1)
                nc.vector.tensor_scalar(second[:, t, :], expert_id, top_idf[:, t, 1:2], e2[:, t:t + 1],
                                        ALU.is_equal, ALU.mult).then_inc(second_set, 1)

            def join_picks(t):
                dve.wait_ge(den_set, t + 1)
                nc.vector.reciprocal(g1[:, t:t + 1], den[:, t:t + 1]).then_inc(g1_set, 1)
                dve.wait_ge(first_set, t + 1)
                dve.wait_ge(second_set, t + 1)
                nc.vector.tensor_tensor(picks[:, t, :], first[:, t, :], second[:, t, :],
                                        ALU.add).then_inc(picks_set, 1)

            def gates(t):
                dve.wait_ge(picks_set, t + 1)
                dve.wait_ge(g1_set, t + 1)
                dve.wait_ge(rstd_t_set, t + 1)
                nc.vector.tensor_scalar(gate_rstd[:, t, :], picks[:, t, :], g1[:, t:t + 1],
                                        rstd_t[:, t:t + 1], ALU.mult, ALU.mult).then_inc(gate_rstd_set, 1)
                nc.vector.tensor_scalar(gate[:, t, :], picks[:, t, :], g1[:, t:t + 1], None,
                                        ALU.mult).then_inc(gate_set, 1)

            def add_expert(t, e):
                dve.wait_ge(gate_rstd_set, t + 1)
                dve.wait_ge(y_ready[t], e + 1)
                if step[t][e] > 1:
                    dve.wait_ge(summed[t], step[t][e] - 1)
                nc.vector.scalar_tensor_tensor(
                    out=total[:, t, :], in0=y_ps[t][e], scalar=gate_rstd[:, t, e:e + 1],
                    in1=(total if step[t][e] > 1 else x1)[:, t, :],
                    op0=ALU.mult, op1=ALU.add).then_inc(summed[t], 1)

            def join(t):
                dve.wait_ge(aside_sum[t], 2)
                dve.wait_ge(summed[t], step[t]["join"] - 1)
                nc.vector.tensor_tensor(total[:, t, :], total[:, t, :], aside[:, t, 0, :],
                                        ALU.add).then_inc(summed[t], 1)

            scan(0)
            residual(0)
            token_center(0)
            scan(1)
            residual(1)
            low_xcT(0)
            token_center(1)
            low_W(2, 0)
            top_logits(0)
            low_W(2, 1)
            low_xcT(1)
            top_ids(0)
            pick_first(0)
            pick_second(0)
            join_picks(0)
            gates(0)
            add_expert(0, 0)
            top_logits(1)
            add_expert(0, 2)
            top_ids(1)
            pick_first(1)
            pick_second(1)
            join_picks(1)
            gates(1)
            add_expert(1, 0)
            for e in (4, 5, 6, 7):
                add_expert(0, e)
            join(0)
            add_expert(1, 3)
            add_expert(1, 4)
            join(1)
            for e in (5, 6, 7):
                add_expert(1, e)


def kernel(**inputs):
    import numpy as np
    import concourse.bacc as bacc
    from concourse.bass_utils import run_bass_kernel_spmd

    def given(name):
        return np.ascontiguousarray(inputs[name])

    x = given("x")
    _, C, R, _ = x.shape
    T = R * R
    NT, ROWS = T // P, P // R
    We, Wg = given("L0_ffn_We"), given("L0_ffn_Wg")
    E, D, H = We.shape
    at, n_params = param_columns(C, R, E)
    params = np.zeros((P, n_params), np.float32)
    params[:, at["ident"]] = np.eye(P, dtype=np.float32)
    params[:, at["row_mask"]] = np.repeat(np.eye(ROWS, dtype=np.float32), R, axis=0)
    params[:, at["expert_id"]] = np.arange(E, dtype=np.float32)
    for t in range(NT):
        for k, name in enumerate(("L0_conv_ln_w", "L0_conv_ln_b")):
            params[:, at["ln"].start + 2 * t + k] = given(name).reshape(NT, P)[t]
    params[:, at["dt_w"]] = np.tile(given("L0_conv_dt_w").reshape(R, 1), (ROWS, 1))
    params[:, at["dt_b"]].reshape(P, NT, 2, ROWS)[:, :, 1, :] = given("L0_conv_dt_b")[0]
    params[:, at["log_A"]] = given("L0_conv_log_A")
    params[:, at["Wg"]] = Wg.reshape(C // P, P, E).transpose(1, 0, 2).reshape(P, -1)
    arrays = {
        "x_tokens": np.ascontiguousarray(x.reshape(C, T).T),
        "params": params,
        "We_rows": np.ascontiguousarray(We.transpose(1, 0, 2)).reshape(D, E * H),
        "be": given("L0_ffn_be"),
    }

    nc = bacc.Bacc("TRN2", target_bir_lowering=False, num_devices=1)
    dram = {name: nc.dram_tensor(f"in_{name}", a.shape, F32, kind="ExternalInput").ap()
            for name, a in arrays.items()}
    out = nc.dram_tensor("out_tokens", (T, C), F32, kind="ExternalOutput").ap()
    metaformer_block(nc, dram["x_tokens"], dram["params"], dram["We_rows"], dram["be"], out)
    result = run_bass_kernel_spmd(nc, [{f"in_{name}": a for name, a in arrays.items()}], core_ids=[0])
    return np.ascontiguousarray(result.results[0]["out_tokens"].T).reshape(1, C, R, R)
```
